# Optimizing a Trainium2 kernel written in Bass

```python
import numpy as np
import jax
import jax.numpy as jnp

def _softmax(x, axis=-1):
    return jax.nn.softmax(x, axis=axis)

def _gelu(x):
    return jax.nn.gelu(x, approximate=True)

def _silu(x):
    return jax.nn.silu(x)

def _sigmoid(x):
    return jax.nn.sigmoid(x)

def _layernorm(x, axis=-1, eps=1e-05):
    m = jnp.mean(x, axis=axis, keepdims=True)
    v = jnp.var(x, axis=axis, keepdims=True)
    return (x - m) / jnp.sqrt(v + eps)

def _scatter_add(tgt, idx, src, axis=0):
    return tgt.at[idx].add(src)

def _segment_sum(src, seg, n):
    return jax.ops.segment_sum(src, seg, n)
kernel_name = 'mk_seq_postln_d1_jaxref_r8_a51fd0'

def setup_inputs(seed: int=0):
    np.random.seed(seed)
    _w = jnp.asarray

    def _L0_attn_setup():
        import jax, jax.numpy as jnp
        import numpy as np
        INF_APPROX = 1e+30
        ROTARY_BASE = 10000.0
        D_HEAD = 128

        def _rope(x, base=ROTARY_BASE):
            _, length, _, width = x.shape
            half = width // 2
            positions = jnp.arange(length, dtype=x.dtype)
            dims = jnp.arange(half, dtype=x.dtype)
            ang_freqs = jnp.power(base, -dims / half)
            radians = positions[:, None] * ang_freqs[None, :]
            cos = jnp.cos(radians)[None, :, None, :]
            sin = jnp.sin(radians)[None, :, None, :]
            even, odd = jnp.split(x, 2, axis=-1)
            return jnp.concatenate([even * cos - odd * sin, even * sin + odd * cos], axis=-1)
        key = jax.random.key(seed)
        k1, k2, k3, k4, k5 = jax.random.split(key, 5)
        B, T, M, H, D = (2, 512, 128, 8, 128)
        n_layer = 24
        x = jax.random.normal(k1, (B, T, M), dtype=jnp.float32)
        std_qkv = M ** (-0.5)
        std_o = (M * 2 * n_layer) ** (-0.5)
        w_aq = jnp.zeros((M, H, D), dtype=jnp.float32)
        w_ak = std_qkv * jax.random.normal(k3, (M, H, D), dtype=jnp.float32)
        w_av = std_qkv * jax.random.normal(k4, (M, H, D), dtype=jnp.float32)
        w_ao = std_o * jax.random.normal(k5, (H, D, M), dtype=jnp.float32)
        return {'x': x, 'w_aq': w_aq, 'w_ak': w_ak, 'w_av': w_av, 'w_ao': w_ao}
    _L0_attn_in = _L0_attn_setup()

    def _L0_ffn_setup():
        import jax, jax.numpy as jnp
        import numpy as np
        D_IN, D_HID = (128, 512)

        def _ternary(key, shape):
            return jax.random.randint(key, shape, -1, 2).astype(jnp.float32)

        def _tlin(x, w, s):
            return jnp.einsum('bsi,oi->bso', x, w) * s
        key = jax.random.key(seed)
        ks = jax.random.split(key, 12)
        inv = lambda fan: 1.0 / np.sqrt(fan).astype(np.float32)
        return {'x': jax.random.normal(ks[0], (4, 256, D_IN), dtype=jnp.float32), 'w1_w': _ternary(ks[1], (D_HID, D_IN)), 'w1_s': jax.random.uniform(ks[2], (D_HID,), dtype=jnp.float32) * inv(D_IN), 'w2_w': _ternary(ks[3], (D_HID, D_IN)), 'w2_s': jax.random.uniform(ks[4], (D_HID,), dtype=jnp.float32) * inv(D_IN), 'h1_w': _ternary(ks[5], (D_HID, D_HID)), 'h1_s': jax.random.uniform(ks[6], (D_HID,), dtype=jnp.float32) * inv(D_HID), 'h2_w': _ternary(ks[7], (D_HID, D_HID)), 'h2_s': jax.random.uniform(ks[8], (D_HID,), dtype=jnp.float32) * inv(D_HID), 'w3_w': _ternary(ks[9], (D_IN, D_HID)), 'w3_s': jax.random.uniform(ks[10], (D_IN,), dtype=jnp.float32) * inv(D_HID)}
    _L0_ffn_in = _L0_ffn_setup()
    _d = {'L0_attn_x': _L0_attn_in['x'], 'L0_attn_w_aq': _L0_attn_in['w_aq'], 'L0_attn_w_ak': _L0_attn_in['w_ak'], 'L0_attn_w_av': _L0_attn_in['w_av'], 'L0_attn_w_ao': _L0_attn_in['w_ao'], 'L0_ffn_w1_w': _L0_ffn_in['w1_w'], 'L0_ffn_w1_s': _L0_ffn_in['w1_s'], 'L0_ffn_w2_w': _L0_ffn_in['w2_w'], 'L0_ffn_w2_s': _L0_ffn_in['w2_s'], 'L0_ffn_h1_w': _L0_ffn_in['h1_w'], 'L0_ffn_h1_s': _L0_ffn_in['h1_s'], 'L0_ffn_h2_w': _L0_ffn_in['h2_w'], 'L0_ffn_h2_s': _L0_ffn_in['h2_s'], 'L0_ffn_w3_w': _L0_ffn_in['w3_w'], 'L0_ffn_w3_s': _L0_ffn_in['w3_s']}
    _x0 = _d['L0_attn_x']
    _d['L0_attn_x'] = jax.random.normal(jax.random.fold_in(jax.random.key(seed), 1), (4, 1024, 128), dtype=_x0.dtype)
    del _x0
    return _d

def reference(L0_attn_x, L0_attn_w_aq, L0_attn_w_ak, L0_attn_w_av, L0_attn_w_ao, L0_ffn_w1_w, L0_ffn_w1_s, L0_ffn_w2_w, L0_ffn_w2_s, L0_ffn_h1_w, L0_ffn_h1_s, L0_ffn_h2_w, L0_ffn_h2_s, L0_ffn_w3_w, L0_ffn_w3_s):

    def _L0_attn_ref(x, w_aq, w_ak, w_av, w_ao):
        import jax, jax.numpy as jnp
        import numpy as np
        INF_APPROX = 1e+30
        ROTARY_BASE = 10000.0
        D_HEAD = 128

        def _rope(x, base=ROTARY_BASE):
            _, length, _, width = x.shape
            half = width // 2
            positions = jnp.arange(length, dtype=x.dtype)
            dims = jnp.arange(half, dtype=x.dtype)
            ang_freqs = jnp.power(base, -dims / half)
            radians = positions[:, None] * ang_freqs[None, :]
            cos = jnp.cos(radians)[None, :, None, :]
            sin = jnp.sin(radians)[None, :, None, :]
            even, odd = jnp.split(x, 2, axis=-1)
            return jnp.concatenate([even * cos - odd * sin, even * sin + odd * cos], axis=-1)
        B, T, M = x.shape
        q = jnp.einsum('btm,mhd->bthd', x, w_aq)
        k = jnp.einsum('btm,mhd->bthd', x, w_ak)
        v = jnp.einsum('btm,mhd->bthd', x, w_av)
        q = _rope(q)
        k = _rope(k)
        s = jnp.einsum('bihd,bjhd->bhij', q, k) / D_HEAD
        i = jnp.arange(T)[:, None]
        j = jnp.arange(T)[None, :]
        mask = (i < j).astype(x.dtype)[None, None, :, :]
        s = s - jnp.asarray(INF_APPROX, x.dtype) * mask
        p = jax.nn.softmax(s, axis=-1)
        o = jnp.einsum('bhij,bjhd->bihd', p, v)
        r = jnp.einsum('bihd,hdm->bim', o, w_ao)
        return r

    def _L0_ffn_ref(x, w1_w, w1_s, w2_w, w2_s, h1_w, h1_s, h2_w, h2_s, w3_w, w3_s):
        import jax, jax.numpy as jnp
        import numpy as np
        D_IN, D_HID = (128, 512)

        def _ternary(key, shape):
            return jax.random.randint(key, shape, -1, 2).astype(jnp.float32)

        def _tlin(x, w, s):
            return jnp.einsum('bsi,oi->bso', x, w) * s
        h = jax.nn.silu(_tlin(x, w1_w, w1_s)) * _tlin(x, w2_w, w2_s)
        h = jax.nn.gelu(_tlin(h, h1_w, h1_s), approximate=False)
        h = jax.nn.gelu(_tlin(h, h2_w, h2_s), approximate=False)
        return _tlin(h, w3_w, w3_s)
    x = L0_attn_x
    x = _layernorm(x + _L0_attn_ref(x, L0_attn_w_aq, L0_attn_w_ak, L0_attn_w_av, L0_attn_w_ao), axis=-1)
    x = _layernorm(x + _L0_ffn_ref(x, L0_ffn_w1_w, L0_ffn_w1_s, L0_ffn_w2_w, L0_ffn_w2_s, L0_ffn_h1_w, L0_ffn_h1_s, L0_ffn_h2_w, L0_ffn_h2_s, L0_ffn_w3_w, L0_ffn_w3_s), axis=-1)
    return x

_drawn_inputs = setup_inputs


def setup_inputs(seed=0):
    import zlib

    import numpy as np

    out = dict(_drawn_inputs(seed))
    spreads = {'L0_attn_w_aq': (0.0, 0.8)}
    factors = {'L0_attn_w_ak': 8.0,
     'L0_ffn_w1_w': 8.0,
     'L0_ffn_w1_s': 8.0,
     'L0_ffn_w2_w': 8.0,
     'L0_ffn_w2_s': 8.0,
     'L0_ffn_h1_w': 8.0,
     'L0_ffn_h1_s': 8.0,
     'L0_ffn_h2_w': 8.0,
     'L0_ffn_h2_s': 8.0,
     'L0_ffn_w3_w': 8.0,
     'L0_ffn_w3_s': 8.0}
    for name, (base, spread) in spreads.items():
        noise = np.random.default_rng([zlib.crc32(name.encode()), seed]).standard_normal(out[name].shape)
        drawn = base * np.exp(spread * noise) if base else spread * noise
        out[name] = jnp.asarray(drawn.astype(out[name].dtype))
    for name, factor in factors.items():
        out[name] = (out[name] * factor).astype(out[name].dtype)
    return out
```

```python
from contextlib import ExitStack

import concourse.bass as bass
import numpy as np
from concourse import mybir

F32 = mybir.dt.float32
F32R = mybir.dt.float32r
ACT = mybir.ActivationFunctionType
ALU = mybir.AluOpType
AX = mybir.AxisListType

B, T, M = 4, 1024, 128
H, D = 8, 128
HID = 512
P = 128
BANK = 512
HEADS = B * H
PAIRS = HEADS // 2
NI = T // P
CHUNKS = T // BANK
TOKENS = B * T
BLOCKS = TOKENS // P
HT = HID // P
EPS = 1e-5
SCORE_SCALE = 1.0 / D
MASKED = -1e30
QH, QL, KH, KL, VH, VL = range(6)

ROPE_TILES = [(0, 0), (1, 0), (0, 1), (1, 1)]
FILLS_OF = [1 if i < 4 else 2 for i in range(NI)]
FIRST_FILL = [sum(FILLS_OF[:i]) for i in range(NI)]
NT = sum(FILLS_OF)
NPROJ = 6
RING = []
for _i in range(NI):
    RING += [("t", FIRST_FILL[_i] + _k) for _k in range(FILLS_OF[_i])]
    if _i < NPROJ:
        RING.append(("p", _i))
RING_BANKS = 3
assert len(RING) % RING_BANKS == 0
PV1_PIECES = {1: range(0, 2), 2: range(2, 4), 3: range(4, 8)}
PV0_PIECES = {5: range(0, 1), 6: range(1, 3), 7: range(3, 4)}


def build(nc, xT, x_tok, w_q, w_k, w_vT, w_o, rope, ident_in, mask_in, f1, f2, g1, g2, f3, scales, out):
    x_split = nc.dram_tensor("x_split", (B, P, 2, T), F32, kind="Internal").ap()
    ctx = ExitStack()
    with ctx:
        def sem(name):
            return ctx.enter_context(nc.semaphore(name))

        rT = ctx.enter_context(nc.sbuf_tensor("rT", [P, TOKENS], F32))
        ident = ctx.enter_context(nc.sbuf_tensor("ident", [P, P], F32))
        attn = ctx.enter_context(ExitStack())
        attention(nc, attn, sem, rT, ident, x_split, xT, w_q, w_k, w_vT, w_o, rope, ident_in, mask_in)
        attn.close()
        feed_forward(nc, ctx, sem, rT, ident, x_tok, f1, f2, g1, g2, f3, scales, out)


def attention(nc, ctx, sem, rT, ident, x_split, xT, w_q, w_k, w_vT, w_o, rope_in, ident_in, mask_in):
    def sb(name, shape, dt=F32, where=ctx):
        return where.enter_context(nc.sbuf_tensor(name, shape, dt))

    rope = sb("rope", [P, 2, T])
    ident_r = sb("ident_r", [P, P], F32R)
    mask_r = sb("mask_r", [P, P], F32R)
    w_all = sb("w_all", [P, H, 6, P], F32R)

    pre = ExitStack()
    raw_x = sb("raw_x", [P, B, T], F32, pre)
    x_parts = sb("x_parts", [P, B, 2, T], F32R, pre)
    raw_w = sb("raw_w", [P, 4, H * P], F32, pre)
    mask_f = sb("mask_f", [P, P], F32, pre)
    warm = sb("warm", [P, 1], F32, pre)
    pvo = pre.enter_context(nc.psum_tensor("pvo", [P, 2 * BANK], F32))

    qk_loaded, vo_loaded, consts_loaded = sem("qk_loaded"), sem("vo_loaded"), sem("consts_loaded")
    x_loaded = [sem(f"x_loaded{b}") for b in range(B)]
    w_high, x_high, x_low, vo_ready = sem("w_high"), sem("x_high"), sem("x_low"), sem("vo_ready")
    x_saved, warm_zero = sem("x_saved"), sem("warm_zero")
    with nc.Block() as block:
        @block.sync
        def _(sp):
            sp.dma_start(raw_w[:, 2], w_vT).then_inc(vo_loaded, 16)
            sp.dma_start(raw_w[:, 3], w_o).then_inc(vo_loaded, 16)
            sp.dma_start(raw_w[:, 0], w_q).then_inc(qk_loaded, 16)
            sp.dma_start(raw_w[:, 1], w_k).then_inc(qk_loaded, 16)
            sp.dma_start(ident[:], ident_in).then_inc(consts_loaded, 16)
            sp.dma_start(mask_f[:], mask_in).then_inc(consts_loaded, 16)
            sp.dma_start(rope[:], rope_in).then_inc(consts_loaded, 16)
            for b in range(B):
                sp.wait_ge(x_low, b + 1)
                sp.dma_start(x_split[b], x_parts[:, b].bitcast(F32)).then_inc(x_saved, 16)
            sp.wait_ge(x_saved, 16 * B)

        @block.gpsimd
        def _(pool):
            nc.gpsimd.memset(warm[:], 0.0).then_inc(warm_zero, 1)
            nc.gpsimd.memset(rT[:], 0.0)

        @block.scalar
        def _(act):
            for b in range(B):
                act.dma_start(raw_x[:, b], xT[:, b * T:(b + 1) * T]).then_inc(x_loaded[b], 16)
            act.wait_ge(warm_zero, 1)
            nc.scalar.activation(warm[:], warm[:], ACT.Exp)
            act.wait_ge(x_loaded[0], 16)
            nc.scalar.activation(x_parts[:, 0, 0], raw_x[:, 0], ACT.Copy).then_inc(x_high, 1)
            act.wait_ge(qk_loaded, 32)
            nc.scalar.activation(w_all[:, :, QH], raw_w[:, 0].rearrange("p (h d) -> p h d", h=H), ACT.Copy,
                                 scale=SCORE_SCALE).then_inc(w_high, 1)
            nc.scalar.activation(w_all[:, :, KH], raw_w[:, 1].rearrange("p (h d) -> p h d", h=H),
                                 ACT.Copy).then_inc(w_high, 1)
            act.wait_ge(vo_ready, 1)
            nc.scalar.activation(w_all[:, :, VH], pvo[:].rearrange("p (h d) -> p h d", h=H),
                                 ACT.Copy).then_inc(w_high, 1)
            for b in range(1, B):
                act.wait_ge(x_loaded[b], 16)
                nc.scalar.activation(x_parts[:, b, 0], raw_x[:, b], ACT.Copy).then_inc(x_high, 1)

        @block.tensor
        def _(pe):
            pe.wait_ge(vo_loaded, 32)
            for h in range(H):
                last = nc.tensor.matmul(pvo[:, h * P:(h + 1) * P], raw_w[:, 2, h * P:(h + 1) * P],
                                        raw_w[:, 3, h * P:(h + 1) * P], start=True, stop=True)
            last.then_inc(vo_ready, 1)

        @block.vector
        def _(dve):
            def x_low_part(b):
                dve.wait_ge(x_high, b + 1)
                nc.vector.tensor_tensor(x_parts[:, b, 1], raw_x[:, b], x_parts[:, b, 0].bitcast(F32),
                                        ALU.subtract).then_inc(x_low, 1)

            x_low_part(0)
            dve.wait_ge(w_high, 1)
            nc.vector.scalar_tensor_tensor(w_all[:, :, QL], raw_w[:, 0].rearrange("p (h d) -> p h d", h=H),
                                           SCORE_SCALE, w_all[:, :, QH].bitcast(F32), ALU.mult, ALU.subtract)
            dve.wait_ge(w_high, 2)
            nc.vector.tensor_tensor(w_all[:, :, KL], raw_w[:, 1].rearrange("p (h d) -> p h d", h=H),
                                    w_all[:, :, KH].bitcast(F32), ALU.subtract)
            dve.wait_ge(w_high, 3)
            nc.vector.tensor_tensor(w_all[:, :, VL], pvo[:].rearrange("p (h d) -> p h d", h=H),
                                    w_all[:, :, VH].bitcast(F32), ALU.subtract)
            dve.wait_ge(consts_loaded, 48)
            nc.vector.tensor_copy(ident_r[:], ident[:])
            nc.vector.tensor_copy(mask_r[:], mask_f[:])
            for b in range(1, B):
                x_low_part(b)
    pre.close()

    w_stage = sb("w_stage", [P, 2, 6, P], F32R)
    x_stage = sb("x_stage", [P, 2, T], F32R)
    qk = sb("qk", [P, 2, 2, 2, T], F32R)
    vals = sb("vals", [P, 2, 2, NI, P], F32R)
    proj = sb("proj", [P, 2, BANK])
    swapped = sb("swapped", [P, 2, BANK])
    by_cos = sb("by_cos", [P, 2, BANK])
    by_sin = sb("by_sin", [P, 2, BANK])
    roped = sb("roped", [P, 2, BANK])
    probs = sb("probs", [P, 4, T])
    pT = [sb("pT0", [P, 2, 4, BANK], F32R), sb("pT1", [P, 2, 8, BANK], F32R)]
    neg_max = sb("neg_max", [P, 2 * NI])
    row_sum = sb("row_sum", [P, 2 * NI])
    inv_sum = sb("inv_sum", [P, 2 * NI])
    score_ps = ctx.enter_context(nc.psum_tensor("score_ps", [P, 2, 2 * BANK], F32))
    ring_ps = ctx.enter_context(nc.psum_tensor("ring_ps", [P, RING_BANKS, BANK], F32))
    pv_ps = ctx.enter_context(nc.psum_tensor("pv_ps", [P, BANK], F32))

    scores_ready = (sem("scores_ready"), NI)
    max_ready = (sem("max_ready"), NI)
    exp_done = (sem("exp_done"), NI)
    inv_ready = (sem("inv_ready"), NI)
    probs_ready = (sem("probs_ready"), NI)
    t_filled = (sem("t_filled"), NT)
    t_high = (sem("t_high"), NT)
    t_low = (sem("t_low"), NT)
    projected = (sem("projected"), NPROJ)
    proj_copied = (sem("proj_copied"), 4)
    cos_done = (sem("cos_done"), 4)
    sin_done = (sem("sin_done"), 4)
    rope_done = (sem("rope_done"), 4)
    rope_high = (sem("rope_high"), 4)
    rope_low = (sem("rope_low"), 4)
    v_high = (sem("v_high"), CHUNKS)
    v_low = (sem("v_low"), CHUNKS)
    pv_done = (sem("pv_done"), CHUNKS)
    pv_added = (sem("pv_added"), CHUNKS)
    swap_done = [(sem("swap_done0"), 64), (sem("swap_done1"), 64)]
    w_staged = [(sem("w_staged0"), 16), (sem("w_staged1"), 16)]
    x_staged, pool_passed, sp_passed = sem("x_staged"), sem("pool_passed"), sem("sp_passed")

    def number(head):
        return 2 * head[0] + head[1]

    def step_on(head, by):
        return head[0], head[1] + by

    def parity(head):
        return head[1] % 2

    def exists(head):
        n = number(head)
        return not isinstance(n, int) or 0 <= n < HEADS

    def wait_for(eng, signal, head, nth):
        semaphore, each = signal
        if exists(head):
            eng.wait_ge(semaphore, each * number(head) + nth + 1)

    def wait_for_swap(eng, head, tile):
        if exists(head):
            eng.wait_ge(swap_done[tile % 2][0], 64 * number(head) + 32 * (tile // 2 + 1))

    def earlier(head, nth, by, each):
        return step_on(head, (nth - by) // each), (nth - by) % each

    def run_pairs(eng, pair_body):
        pair_body(0)
        with eng.Fori(1, PAIRS - 1) as pair:
            pair_body(pair)
        pair_body(PAIRS - 1)

    def steps(pair, body):
        for off in range(2):
            for s in range(NI):
                body((pair, off), s)

    def bank_of(kind, nth):
        return RING.index((kind, nth)) % RING_BANKS

    def wait_ring_bank(pe, kind, nth, head):
        at = RING.index((kind, nth))
        prev_head, prev = earlier(head, at, RING_BANKS, len(RING))
        if number(head) == -1 if isinstance(number(head), int) else False:
            while exists(step_on(prev_head, 1)) and RING[prev][0] == "t":
                prev_head, prev = earlier(prev_head, prev, RING_BANKS, len(RING))
            if number(prev_head) < -1:
                return
        user, n = RING[prev]
        if user == "t":
            wait_for(pe, t_low, prev_head, n)
        elif n < 4:
            wait_for(pe, proj_copied, step_on(prev_head, 1), n)
        else:
            wait_for(pe, v_low, step_on(prev_head, 1), n - 4)

    def split_products(out_ap, left, right, first, last):
        terms = ((0, 0), (0, 1), (1, 0))
        for i, (a, b) in enumerate(terms):
            ins = nc.tensor.matmul(out_ap, left[a], right[b], start=first and i == 0, stop=last and i == 2)
        return ins

    with nc.Block() as block:
        @block.sync
        def _(sp):
            def stage_x(b):
                if not isinstance(b, int) or b > 0:
                    sp.wait_ge(projected[0], NPROJ * H * b)
                sp.dma_start(x_stage[:].bitcast(F32), x_split[b] if isinstance(b, int) else x_split[bass.ds(b, 1)].rearrange(
                    "o p a t -> p (o a) t")).then_inc(x_staged, 16)
                sp.wait_ge(x_staged, 16 * b + 16)
                sp.sem_inc(sp_passed, 1)

            def stage_head(b, hp, q):
                head = (4 * b + hp, q)
                src = w_all[:, 2 * hp + q] if isinstance(hp, int) else w_all[:, bass.ds(sp.snap(2 * hp + q), 1)].rearrange(
                    "p o k d -> p (o k) d")
                wait_for(sp, projected, step_on(head, -2), NPROJ - 1)
                sp.dma_start(w_stage[:, q].bitcast(F32), src.bitcast(F32)).then_inc(w_staged[q][0], 16)
                for j in range(4):
                    wait_for(sp, proj_copied, head, j)
                    for lo, hi in ((0, 64), (64, 0)):
                        sp.dma_start(swapped[lo:lo + 64, j % 2], proj[hi:hi + 64, j % 2]).then_inc(
                            swap_done[j % 2][0], 16)

            stage_x(0)
            for q in range(2):
                stage_head(0, 0, q)
            with sp.Fori(1, H // 2) as hp:
                for q in range(2):
                    stage_head(0, hp, q)
            with sp.Fori(1, B) as b:
                stage_x(b)
                with sp.Fori(0, H // 2) as hp:
                    for q in range(2):
                        stage_head(b, hp, q)

        @block.tensor
        def _(pe):
            def scores(head, ib):
                wait_for(pe, rope_low, head, 1 if ib < 4 else 3)
                wait_for(pe, exp_done, *earlier(head, ib, 2, NI))
                q, k = ([qk[:, parity(head), which, part] for part in range(2)] for which in range(2))
                width = (ib + 1) * P
                for c0 in range(0, width, BANK):
                    cols = slice(c0, min(c0 + BANK, width))
                    dst = score_ps[:, ib % 2, cols]
                    left = [a[:, ib * P:(ib + 1) * P] for a in q]
                    right = [a[:, cols] for a in k]
                    nc.tensor.matmul(dst, left[0], right[0], start=True, stop=False)
                    if cols.stop == width:
                        nc.tensor.matmul(score_ps[:, ib % 2, width - P:width], ident_r[:], mask_r[:],
                                         start=False, stop=False)
                    nc.tensor.matmul(dst, left[0], right[1], start=False, stop=False)
                    last = nc.tensor.matmul(dst, left[1], right[0], start=False, stop=True)
                last.then_inc(scores_ready[0], 1)

            def transpose_probs(head, ib):
                wait_for(pe, probs_ready, head, ib)
                for f in range(FILLS_OF[ib]):
                    nth = FIRST_FILL[ib] + f
                    wait_ring_bank(pe, "t", nth, head)
                    for jb in range(4 * f, min(4 * f + 4, ib + 1)):
                        last = nc.tensor.transpose(ring_ps[:, bank_of("t", nth), (jb % 4) * P:(jb % 4 + 1) * P],
                                                   probs[:, ib % 4, jb * P:(jb + 1) * P], ident[:])
                    last.then_inc(t_filled[0], 1)

            def project(running, nth):
                head = step_on(running, 1)
                if nth == 0:
                    pe.wait_ge(w_staged[parity(head)][0], 16 * (head[0] + head[1] // 2) + 16)
                wait_ring_bank(pe, "p", nth, running)
                w = w_stage[:, parity(head)]
                bank = bank_of("p", nth)
                if nth < 4:
                    which, c = ROPE_TILES[nth]
                    last = split_products(ring_ps[:, bank], (w[:, QH + 2 * which], w[:, QL + 2 * which]),
                                          [x_stage[:, part, c * BANK:(c + 1) * BANK] for part in range(2)], True, True)
                else:
                    for i in range(4):
                        t0 = (nth - 4) * BANK + i * P
                        last = split_products(ring_ps[:, bank, i * P:(i + 1) * P],
                                              [x_stage[:, part, t0:t0 + P] for part in range(2)],
                                              (w[:, VH], w[:, VL]), True, True)
                last.then_inc(projected[0], 1)

            def attend(head, chunk, key_blocks):
                if key_blocks[0] == 0:
                    wait_for(pe, t_low, head, NT - 1 if chunk else 3)
                    wait_for(pe, v_low, head, CHUNKS - 1)
                    wait_for(pe, pv_added, *earlier(head, chunk, 1, CHUNKS))
                for jb in key_blocks:
                    i0 = max(0, jb * P - chunk * BANK)
                    last = split_products(pv_ps[:, i0:], [vals[:, parity(head), part, jb] for part in range(2)],
                                          [pT[chunk][:, part, jb, i0:] for part in range(2)],
                                          jb == 0, jb == 4 * chunk + 3)
                if key_blocks[-1] == 4 * chunk + 3:
                    last.then_inc(pv_done[0], 1)

            def step(head, s):
                ahead = step_on(head, (s + 2) // NI)
                if exists(ahead):
                    scores(ahead, (s + 2) % NI)
                transpose_probs(head, s)
                if s < NPROJ and exists(step_on(head, 1)):
                    project(head, s)
                if s in PV1_PIECES and exists(step_on(head, -1)):
                    attend(step_on(head, -1), 1, PV1_PIECES[s])
                if s in PV0_PIECES:
                    attend(head, 0, PV0_PIECES[s])

            for nth in range(NPROJ):
                project((0, -1), nth)
            scores((0, 0), 0)
            scores((0, 0), 1)
            run_pairs(pe, lambda pair: steps(pair, step))
            attend((PAIRS - 1, 1), 1, range(8))

        @block.scalar
        def _(act):
            def exponentiate(head, ib):
                n = parity(head) * NI + ib
                wait_for(act, max_ready, head, ib)
                old_head, old = earlier(head, ib, 4, NI)
                wait_for(act, t_filled, old_head, FIRST_FILL[old] + FILLS_OF[old] - 1)
                width = (ib + 1) * P
                nc.scalar.activation(probs[:, ib % 4, :width], score_ps[:, ib % 2, :width], ACT.Exp,
                                     bias=neg_max[:, n:n + 1], accum_out=row_sum[:, n:n + 1]).then_inc(exp_done[0], 1)

            def transposed_high(head, ib):
                chunk = ib // 4
                if ib % 4 == 0:
                    wait_for(act, pv_done, step_on(head, -1), chunk)
                for f in range(FILLS_OF[ib]):
                    nth = FIRST_FILL[ib] + f
                    n_blocks = min(4, ib + 1 - 4 * f)
                    wait_for(act, t_filled, head, nth)
                    nc.scalar.activation(
                        pT[chunk][:, 0, 4 * f:4 * f + n_blocks, (ib % 4) * P:(ib % 4 + 1) * P],
                        ring_ps[:, bank_of("t", nth), :n_blocks * P].rearrange("p (j i) -> p j i", i=P),
                        ACT.Copy).then_inc(t_high[0], 1)

            def copy_projected(head, j):
                wait_for(act, projected, head, j)
                old_head, old = earlier(head, j, 2, 4)
                wait_for(act, cos_done, old_head, old)
                wait_for(act, sin_done, old_head, old)
                nc.scalar.activation(proj[:, j % 2], ring_ps[:, bank_of("p", j)], ACT.Copy).then_inc(proj_copied[0], 1)

            def roped_high(head, j):
                which, c = ROPE_TILES[j]
                wait_for(act, rope_done, head, j)
                if j == 0:
                    wait_for(act, scores_ready, step_on(head, -2), NI - 1)
                nc.scalar.activation(qk[:, parity(head), which, 0, c * BANK:(c + 1) * BANK], roped[:, j % 2],
                                     ACT.Copy).then_inc(rope_high[0], 1)

            def values_high(head, c):
                wait_for(act, projected, head, 4 + c)
                if c == 0:
                    wait_for(act, pv_done, step_on(head, -2), 1)
                nc.scalar.activation(vals[:, parity(head), 0, 4 * c:4 * c + 4],
                                     ring_ps[:, bank_of("p", 4 + c)].rearrange("p (j m) -> p j m", m=P),
                                     ACT.Copy).then_inc(v_high[0], 1)

            def step(head, s):
                nxt = step_on(head, 1)
                ahead = step_on(head, (s + 1) // NI)
                if exists(ahead):
                    exponentiate(ahead, (s + 1) % NI)
                if exists(nxt) and 3 <= s < 7:
                    roped_high(nxt, s - 3)
                transposed_high(head, s)
                if exists(nxt) and s < 4:
                    copy_projected(nxt, s)
                if exists(nxt) and 4 <= s < 6:
                    values_high(nxt, s - 4)

            for j in range(4):
                copy_projected((0, 0), j)
            for c in range(CHUNKS):
                values_high((0, 0), c)
            for j in range(4):
                roped_high((0, 0), j)
            exponentiate((0, 0), 0)
            run_pairs(act, lambda pair: steps(pair, step))

        @block.vector
        def _(dve):
            def negative_max(head, ib):
                n = parity(head) * NI + ib
                wait_for(dve, scores_ready, head, ib)
                nc.vector.tensor_reduce(neg_max[:, n:n + 1], score_ps[:, ib % 2, :(ib + 1) * P], AX.X, ALU.max,
                                        negate=True).then_inc(max_ready[0], 1)

            def inverse_sum(head, ib):
                n = parity(head) * NI + ib
                wait_for(dve, exp_done, head, ib)
                nc.vector.reciprocal(inv_sum[:, n:n + 1], row_sum[:, n:n + 1]).then_inc(inv_ready[0], 1)

            def transposed_low(head, ib):
                chunk = ib // 4
                for f in range(FILLS_OF[ib]):
                    nth = FIRST_FILL[ib] + f
                    n_blocks = min(4, ib + 1 - 4 * f)
                    high, low = (pT[chunk][:, part, 4 * f:4 * f + n_blocks, (ib % 4) * P:(ib % 4 + 1) * P]
                                 for part in range(2))
                    wait_for(dve, t_high, head, nth)
                    nc.vector.tensor_tensor(
                        low, ring_ps[:, bank_of("t", nth), :n_blocks * P].rearrange("p (j i) -> p j i", i=P),
                        high.bitcast(F32), ALU.subtract).then_inc(t_low[0], 1)

            def times_cos(head, j):
                c = ROPE_TILES[j][1]
                wait_for(dve, proj_copied, head, j)
                wait_for(dve, rope_done, *earlier(head, j, 2, 4))
                nc.vector.tensor_tensor(by_cos[:, j % 2], proj[:, j % 2], rope[:, 0, c * BANK:(c + 1) * BANK],
                                        ALU.mult).then_inc(cos_done[0], 1)

            def add_rope(head, j):
                wait_for(dve, cos_done, head, j)
                wait_for(dve, sin_done, head, j)
                wait_for(dve, rope_low, *earlier(head, j, 2, 4))
                nc.vector.tensor_tensor(roped[:, j % 2], by_cos[:, j % 2], by_sin[:, j % 2],
                                        ALU.add).then_inc(rope_done[0], 1)

            def values_low(head, c):
                high, low = (vals[:, parity(head), part, 4 * c:4 * c + 4] for part in range(2))
                wait_for(dve, v_high, head, c)
                nc.vector.tensor_tensor(low, ring_ps[:, bank_of("p", 4 + c)].rearrange("p (j m) -> p j m", m=P),
                                        high.bitcast(F32), ALU.subtract).then_inc(v_low[0], 1)

            def add_head(head, chunk):
                if not exists(head):
                    return
                col = number(head) // H * T + chunk * BANK
                acc = rT[:, bass.ds(col, BANK)] if not isinstance(col, int) else rT[:, col:col + BANK]
                wait_for(dve, pv_done, head, chunk)
                wait_for(dve, pv_added, *earlier(head, chunk, 2, CHUNKS))
                nc.vector.tensor_tensor(acc, pv_ps[:], acc, ALU.add).then_inc(pv_added[0], 1)

            def step(head, s):
                nxt = step_on(head, 1)
                ahead = step_on(head, (s + 1) // NI)
                if exists(ahead):
                    negative_max(ahead, (s + 1) % NI)
                if s == 0:
                    add_head(step_on(head, -1), 0)
                if s == 4:
                    add_head(step_on(head, -1), 1)
                if exists(nxt) and 1 <= s < 5:
                    times_cos(nxt, s - 1)
                if exists(nxt) and 2 <= s < 6:
                    add_rope(nxt, s - 2)
                if exists(ahead):
                    inverse_sum(ahead, (s + 1) % NI)
                transposed_low(head, s)
                if exists(nxt) and 4 <= s < 6:
                    values_low(nxt, s - 4)

            first = (0, 0)
            times_cos(first, 0)
            times_cos(first, 1)
            add_rope(first, 0)
            times_cos(first, 2)
            add_rope(first, 1)
            times_cos(first, 3)
            values_low(first, 0)
            values_low(first, 1)
            add_rope(first, 2)
            add_rope(first, 3)
            negative_max(first, 0)
            inverse_sum(first, 0)
            run_pairs(dve, lambda pair: steps(pair, step))
            add_head((PAIRS - 1, 1), 0)
            add_head((PAIRS - 1, 1), 1)

        @block.gpsimd
        def _(pool):
            def normalize(head, ib):
                n = parity(head) * NI + ib
                wait_for(pool, inv_ready, head, ib)
                pool.sem_inc(pool_passed, 1)
                p = probs[:, ib % 4, :(ib + 1) * P]
                nc.gpsimd.tensor_scalar(p, p, inv_sum[:, n:n + 1], 1.0, ALU.mult, ALU.mult).then_inc(probs_ready[0], 1)

            def times_sin(head, j):
                c = ROPE_TILES[j][1]
                wait_for_swap(pool, head, j)
                wait_for(pool, rope_done, *earlier(head, j, 2, 4))
                nc.gpsimd.tensor_tensor(by_sin[:, j % 2], swapped[:, j % 2], rope[:, 1, c * BANK:(c + 1) * BANK],
                                        ALU.mult).then_inc(sin_done[0], 1)

            def roped_low(head, j):
                which, c = ROPE_TILES[j]
                high, low = (qk[:, parity(head), which, part, c * BANK:(c + 1) * BANK] for part in range(2))
                wait_for(pool, rope_high, head, j)
                nc.gpsimd.tensor_tensor(low, roped[:, j % 2], high.bitcast(F32), ALU.subtract).then_inc(rope_low[0], 1)

            def step(head, s):
                nxt = step_on(head, 1)
                ahead = step_on(head, (s + 1) // NI)
                if exists(nxt) and 1 <= s < 5:
                    times_sin(nxt, s - 1)
                if exists(ahead):
                    normalize(ahead, (s + 1) % NI)
                if exists(nxt) and 3 <= s < 7:
                    roped_low(nxt, s - 3)

            first = (0, 0)
            times_sin(first, 0)
            times_sin(first, 1)
            roped_low(first, 0)
            times_sin(first, 2)
            roped_low(first, 1)
            times_sin(first, 3)
            roped_low(first, 2)
            roped_low(first, 3)
            normalize(first, 0)
            run_pairs(pool, lambda pair: steps(pair, step))


def feed_forward(nc, ctx, sem, rT, ident, x_tok, f1, f2, g1, g2, f3, scales_in, out):
    def sb(name, shape, dt=F32, where=ctx):
        return where.enter_context(nc.sbuf_tensor(name, shape, dt))

    CH = TOKENS // BANK
    PER = BANK // P
    WCOLS = 2 * HID + 2 * HT * HID + HT * M
    y = sb("y", [P, BLOCKS, M])
    w = sb("w", [P, 2, WCOLS], F32R)
    scales = sb("scales", [P, 4 * HT + 1])
    stats = sb("stats", [P, BLOCKS, 6])
    mean_var = sb("mean_var", [P, BLOCKS, 2])
    rstd = sb("rstd", [P, BLOCKS])
    shift = sb("shift", [P, BLOCKS])
    eps = sb("eps", [P, 1])
    y_loaded, w_loaded, s_loaded, w_high, w_ready = (sem(n) for n in ("y_loaded", "ffn_loaded", "s_loaded", "ffn_high", "ffn_ready"))
    r_turned, r_added, stat_done, aggregated, sqrt_done, norm_ready = (
        sem(n) for n in ("r_turned", "r_added", "stat_done", "aggregated", "sqrt_done", "norm_ready"))
    eps_set = sem("eps_set")

    def w_at(base, part, k, o):
        return w[:, part, base + k + o:base + k + o + P]

    F1, F2, G1, G2, F3 = 0, HID, 2 * HID, 2 * HID + HT * HID, 2 * HID + 2 * HT * HID
    S1, S2, SG1, SG2, S3 = 0, HT, 2 * HT, 3 * HT, 4 * HT

    pre = ExitStack()
    raw = sb("raw", [P, WCOLS], F32, pre)
    turn_ps = pre.enter_context(nc.psum_tensor("turn_ps", [P, 2, BANK], F32))
    with nc.Block() as block:
        @block.sync
        def _(sp):
            sp.dma_start(y[:], x_tok).then_inc(y_loaded, 16)
            for base, src, cols in ((F1, f1, HID), (F2, f2, HID), (G1, g1, HT * HID), (G2, g2, HT * HID), (F3, f3, HT * M)):
                sp.dma_start(raw[:, base:base + cols], src).then_inc(w_loaded, 16)
            sp.dma_start(scales[:], scales_in).then_inc(s_loaded, 16)

        @block.tensor
        def _(pe):
            for c in range(CH):
                if c >= 2:
                    pe.wait_ge(r_added, c - 1)
                for i in range(PER):
                    t0 = c * BANK + i * P
                    last = nc.tensor.transpose(turn_ps[:, c % 2, i * P:(i + 1) * P], rT[:, t0:t0 + P], ident[:])
                last.then_inc(r_turned, 1)

        @block.gpsimd
        def _(pool):
            nc.gpsimd.memset(eps[:], EPS).then_inc(eps_set, 1)
            pool.wait_ge(w_high, 1)
            nc.gpsimd.tensor_tensor(w[:, 1], raw[:], w[:, 0].bitcast(F32), ALU.subtract).then_inc(w_ready, 1)

        @block.vector
        def _(dve):
            dve.wait_ge(y_loaded, 16)
            for c in range(CH):
                blocks = y[:, c * PER:(c + 1) * PER].rearrange("p b m -> p (b m)")
                dve.wait_ge(r_turned, c + 1)
                nc.vector.tensor_tensor(blocks, turn_ps[:, c % 2], blocks, ALU.add).then_inc(r_added, 1)
                dve.wait_ge(r_added, c + 1)
                for i in range(PER):
                    n = c * PER + i
                    nc.vector.bn_stats(stats[:, n], y[:, n]).then_inc(stat_done, 1)
            for n in range(BLOCKS):
                dve.wait_ge(stat_done, n + 1)
                last = nc.vector.bn_aggr(mean_var[:, n], stats[:, n])
            last.then_inc(aggregated, 1)
            dve.wait_ge(sqrt_done, 1)
            nc.vector.reciprocal(rstd[:], shift[:]).then_inc(norm_ready, 1)
            dve.wait_ge(norm_ready, 1)
            nc.vector.scalar_tensor_tensor(shift[:], mean_var[:, :, 0], -1.0, rstd[:], ALU.mult,
                                           ALU.mult).then_inc(norm_ready, 1)
            dve.wait_ge(s_loaded, 16)

        @block.scalar
        def _(act):
            act.wait_ge(w_loaded, 80)
            nc.scalar.activation(w[:, 0], raw[:], ACT.Copy).then_inc(w_high, 1)
            act.wait_ge(eps_set, 1)
            act.wait_ge(aggregated, 1)
            nc.scalar.activation(shift[:], mean_var[:, :, 1], ACT.Sqrt, bias=eps[:]).then_inc(sqrt_done, 1)
    pre.close()

    y_norm = sb("y_norm", [P, 2, PER, M])
    yT = sb("yT", [P, 2, 2, BANK], F32R)
    hid = sb("hid", [P, 2, 2, 2, HT, BANK], F32R)
    gate = sb("gate", [P, 2, BANK])
    value = sb("value", [P, 2, BANK])
    outT = sb("outT", [P, 2, BANK])
    ps = ctx.enter_context(nc.psum_tensor("ps", [P, 2, HT, BANK], F32))
    y_ready, y_turned, yT_high, yT_low = ((sem(n), 1) for n in ("y_ready", "y_turned", "yT_high", "yT_low"))
    y_ready = (y_ready[0], 1)
    gated_filled, gate_done, value_done, hid_high, hid_low = (sem(n) for n in ("gated_filled", "gate_done", "value_done", "hid_high", "hid_low"))
    layer_filled, gelu_done, out_filled, out_copied, out_turned, y_summed = (
        sem(n) for n in ("layer_filled", "gelu_done", "out_filled", "out_copied", "out_turned", "y_summed"))
    sqrt2, norm2, out_ready, stored = sem("sqrt2"), sem("norm2"), sem("out_ready"), sem("stored")
    PAIRS_OF_CHUNKS = CH // 2

    def count(pair, each_pair, nth):
        return each_pair * pair + nth + 1

    with nc.Block() as block:
        @block.tensor
        def _(pe):
            def body(pair):
                for c in range(2):
                    pe.wait_ge(y_ready[0], count(pair, 2, c))
                    if not isinstance(pair, int):
                        pe.wait_ge(y_summed, count(pair, 2, c - 2))
                    for i in range(PER):
                        last = nc.tensor.transpose(ps[:, c, 0, i * P:(i + 1) * P], y_norm[:, c, i], ident[:])
                    last.then_inc(y_turned[0], 1)
                for c in range(2):
                    pe.wait_ge(yT_low[0], count(pair, 2, c))
                    for o in range(HT):
                        if o >= 2:
                            pe.wait_ge(value_done, count(pair, 2 * HT, c * HT + o - 2))
                        for n, base in enumerate((F1, F2)):
                            for i, (a, b) in enumerate(((0, 0), (0, 1), (1, 0))):
                                last = nc.tensor.matmul(ps[:, c, 2 * (o % 2) + n], w_at(base, a, 0, o * P), yT[:, c, b],
                                                        start=i == 0, stop=i == 2)
                        last.then_inc(gated_filled, 1)
                for layer, base in enumerate((G1, G2)):
                    for c in range(2):
                        if layer == 0:
                            pe.wait_ge(value_done, count(pair, 2 * HT, c * HT + HT - 1))
                        for k in range(HT):
                            pe.wait_ge(hid_low, count(pair, 6 * HT, (2 * layer + c) * HT + k))
                            if layer == 1 and k == 0:
                                pe.wait_ge(gelu_done, count(pair, 4 * HT, c * HT + HT - 1))
                            for o in range(HT):
                                for i, (a, b) in enumerate(((0, 0), (0, 1), (1, 0))):
                                    last = nc.tensor.matmul(ps[:, c, o], w_at(base, a, k * HID, o * P), hid[:, c, layer, b, k],
                                                            start=k == 0 and i == 0, stop=k == HT - 1 and i == 2)
                                if k == HT - 1:
                                    last.then_inc(layer_filled, 1)
                for c in range(2):
                    pe.wait_ge(gelu_done, count(pair, 4 * HT, (2 + c) * HT + HT - 1))
                    for k in range(HT):
                        pe.wait_ge(hid_low, count(pair, 6 * HT, (4 + c) * HT + k))
                        for i, (a, b) in enumerate(((0, 0), (0, 1), (1, 0))):
                            last = nc.tensor.matmul(ps[:, c, 0], w_at(F3, a, k * M, 0), hid[:, c, 0, b, k],
                                                    start=k == 0 and i == 0, stop=k == HT - 1 and i == 2)
                    last.then_inc(out_filled, 1)
                for c in range(2):
                    pe.wait_ge(out_copied, count(pair, 2, c))
                    for i in range(PER):
                        last = nc.tensor.transpose(ps[:, c, 1, i * P:(i + 1) * P], outT[:, c, i * P:(i + 1) * P], ident[:])
                    last.then_inc(out_turned, 1)

            body(0)
            with pe.Fori(1, PAIRS_OF_CHUNKS) as pair:
                body(pair)

        @block.vector
        def _(dve):
            def body(pair):
                first = isinstance(pair, int)
                for c in range(2):
                    block0 = (2 * pair + c) * PER
                    if not first:
                        dve.wait_ge(y_summed, count(pair, 2, c - 2))
                    for i in range(PER):
                        src, a, b = ((t[:, bass.ds(block0 + i, 1)] if not first else t[:, block0 + i:block0 + i + 1])
                                     for t in (y, rstd, shift))
                        last = nc.vector.tensor_scalar(y_norm[:, c, i], src.rearrange("p o m -> p (o m)"), a, b,
                                                       ALU.mult, ALU.add)
                    last.then_inc(y_ready[0], 1)
                for c in range(2):
                    dve.wait_ge(yT_high[0], count(pair, 2, c))
                    nc.vector.tensor_tensor(yT[:, c, 1], ps[:, c, 0], yT[:, c, 0].bitcast(F32), ALU.subtract).then_inc(yT_low[0], 1)

                def low(layer2, c, o, nth):
                    dve.wait_ge(hid_high, count(pair, 6 * HT, nth))
                    nc.vector.tensor_tensor(hid[:, c, layer2, 1, o], value[:, o % 2], hid[:, c, layer2, 0, o].bitcast(F32),
                                            ALU.subtract).then_inc(hid_low, 1)

                for c in range(2):
                    for o in range(HT):
                        nth = c * HT + o
                        dve.wait_ge(gate_done, count(pair, 2 * HT, nth))
                        if not (first and nth < 2):
                            dve.wait_ge(hid_low, count(pair, 6 * HT, nth - 2))
                        nc.vector.scalar_tensor_tensor(value[:, o % 2], ps[:, c, 2 * (o % 2) + 1], scales[:, S2 + o:S2 + o + 1],
                                                       gate[:, o % 2], ALU.mult, ALU.mult).then_inc(value_done, 1)
                        low(0, c, o, nth)
                for layer in range(2):
                    for c in range(2):
                        for o in range(HT):
                            nth = (2 * layer + c) * HT + o
                            dve.wait_ge(gelu_done, count(pair, 4 * HT, nth))
                            nc.vector.tensor_copy(hid[:, c, 1 - layer, 0, o], value[:, o % 2]).then_inc(hid_high, 1)
                            low(1 - layer, c, o, 2 * HT + nth)
                for c in range(2):
                    dve.wait_ge(out_turned, count(pair, 2, c))
                    dst = y[:, bass.ds((2 * pair + c) * PER, PER)] if not first else y[:, c * PER:(c + 1) * PER]
                    nc.vector.tensor_tensor(dst.rearrange("p b m -> p (b m)"), ps[:, c, 1],
                                            y_norm[:, c].rearrange("p b m -> p (b m)"), ALU.add).then_inc(y_summed, 1)

            body(0)
            with dve.Fori(1, PAIRS_OF_CHUNKS) as pair:
                body(pair)
            dve.wait_ge(y_summed, CH)
            for n in range(BLOCKS):
                nc.vector.bn_stats(stats[:, n], y[:, n]).then_inc(stat_done, 1)
            for n in range(BLOCKS):
                dve.wait_ge(stat_done, BLOCKS + n + 1)
                last = nc.vector.bn_aggr(mean_var[:, n], stats[:, n])
            last.then_inc(aggregated, 1)
            dve.wait_ge(sqrt2, 1)
            nc.vector.reciprocal(rstd[:], shift[:]).then_inc(norm2, 1)
            dve.wait_ge(norm2, 1)
            nc.vector.scalar_tensor_tensor(shift[:], mean_var[:, :, 0], -1.0, rstd[:], ALU.mult, ALU.mult).then_inc(norm2, 1)
            dve.wait_ge(norm2, 2)
            for n in range(BLOCKS):
                nc.vector.tensor_scalar(y[:, n], y[:, n], rstd[:, n:n + 1], shift[:, n:n + 1], ALU.mult,
                                        ALU.add).then_inc(out_ready, 1)

        @block.scalar
        def _(act):
            def body(pair):
                first = isinstance(pair, int)
                for c in range(2):
                    act.wait_ge(y_turned[0], count(pair, 2, c))
                    nc.scalar.activation(yT[:, c, 0], ps[:, c, 0], ACT.Copy).then_inc(yT_high[0], 1)
                for c in range(2):
                    for o in range(HT):
                        nth = c * HT + o
                        act.wait_ge(gated_filled, count(pair, 2 * HT, nth))
                        if not (first and nth < 2):
                            act.wait_ge(value_done, count(pair, 2 * HT, nth - 2))
                        nc.scalar.activation(gate[:, o % 2], ps[:, c, 2 * (o % 2)], ACT.Silu,
                                             scale=scales[:, S1 + o:S1 + o + 1]).then_inc(gate_done, 1)
                        act.wait_ge(value_done, count(pair, 2 * HT, nth))
                        nc.scalar.activation(hid[:, c, 0, 0, o], value[:, o % 2], ACT.Copy).then_inc(hid_high, 1)
                for layer, s in enumerate((SG1, SG2)):
                    for c in range(2):
                        for o in range(HT):
                            nth = (2 * layer + c) * HT + o
                            act.wait_ge(layer_filled, count(pair, 4 * HT, nth))
                            act.wait_ge(hid_low, count(pair, 6 * HT, 2 * HT + nth - 2))
                            nc.scalar.activation(value[:, o % 2], ps[:, c, o], ACT.Gelu,
                                                 scale=scales[:, s + o:s + o + 1]).then_inc(gelu_done, 1)
                for c in range(2):
                    act.wait_ge(out_filled, count(pair, 2, c))
                    nc.scalar.activation(outT[:, c], ps[:, c, 0], ACT.Copy, scale=scales[:, S3:S3 + 1]).then_inc(out_copied, 1)

            body(0)
            with act.Fori(1, PAIRS_OF_CHUNKS) as pair:
                body(pair)
            act.wait_ge(aggregated, 2)
            nc.scalar.activation(shift[:], mean_var[:, :, 1], ACT.Sqrt, bias=eps[:]).then_inc(sqrt2, 1)

        @block.sync
        def _(sp):
            for c in range(CH):
                sp.wait_ge(out_ready, (c + 1) * PER)
                sp.dma_start(out[:, c * PER:(c + 1) * PER], y[:, c * PER:(c + 1) * PER]).then_inc(stored, 16)
            sp.wait_ge(stored, 16 * CH)


def kernel(**inputs):
    import concourse.bacc as bacc
    from concourse.bass_utils import run_bass_kernel_spmd

    def take(name):
        return np.asarray(inputs["L0_" + name])

    def c(a):
        return np.ascontiguousarray(a)

    half = D // 2
    freq = np.power(np.float32(10000.0), -np.arange(half, dtype=np.float32) / np.float32(half)).astype(np.float32)
    angle = (np.arange(T, dtype=np.float32)[None, :] * freq[:, None]).astype(np.float32).astype(np.float64)
    cos, sin = np.cos(angle), np.sin(angle)
    rope = np.stack([np.concatenate([cos, cos]), np.concatenate([-sin, sin])], axis=1).astype(np.float32)

    def by_tile(a, tiles):
        return a.T.reshape(tiles, P, -1).transpose(1, 0, 2).reshape(P, -1)

    x = take("attn_x").reshape(TOKENS, M)
    scales = np.concatenate([take(n).reshape(-1, P).T for n in ("ffn_w1_s", "ffn_w2_s", "ffn_h1_s", "ffn_h2_s", "ffn_w3_s")], axis=1)
    arrays = {
        "xT": c(x.T),
        "x_tok": c(x.reshape(BLOCKS, P, M).transpose(1, 0, 2)),
        "w_q": c(take("attn_w_aq").reshape(M, H * D)),
        "w_k": c(take("attn_w_ak").reshape(M, H * D)),
        "w_vT": c(take("attn_w_av").transpose(2, 1, 0).reshape(D, H * M)),
        "w_o": c(take("attn_w_ao").transpose(1, 0, 2).reshape(D, H * M)),
        "rope_in": rope,
        "ident_in": np.eye(P, dtype=np.float32),
        "mask_in": np.triu(np.full((P, P), MASKED, np.float32), 1),
        "f1": c(by_tile(take("ffn_w1_w"), 1)),
        "f2": c(by_tile(take("ffn_w2_w"), 1)),
        "g1": c(by_tile(take("ffn_h1_w"), HT)),
        "g2": c(by_tile(take("ffn_h2_w"), HT)),
        "f3": c(by_tile(take("ffn_w3_w"), HT)),
        "scales_in": c(scales),
    }
    nc = bacc.Bacc("TRN2", target_bir_lowering=False, num_devices=1)
    args = [nc.dram_tensor(n, a.shape, mybir.dt.from_np(a.dtype), kind="ExternalInput").ap() for n, a in arrays.items()]
    out = nc.dram_tensor("out", (P, BLOCKS, M), F32, kind="ExternalOutput").ap()
    build(nc, *args, out)
    r = run_bass_kernel_spmd(nc, [arrays], core_ids=[0])
    return r.results[0]["out"].transpose(1, 0, 2).reshape(B, T, M)
```

```python
from contextlib import ExitStack

import concourse.bass as bass
import numpy as np
from concourse import mybir

F32 = mybir.dt.float32
F32R = mybir.dt.float32r
BF16 = mybir.dt.bfloat16
I32 = mybir.dt.int32
ACT = mybir.ActivationFunctionType
ALU = mybir.AluOpType
AX = mybir.AxisListType

B, T, M = 4, 1024, 128
H, D = 8, 128
HID = 512
P = 128
BANK = 512
HEADS = B * H
PAIRS = HEADS // 2
NI = T // P
CHUNKS = T // BANK
TOKENS = B * T
BLOCKS = TOKENS // P
HT = HID // P
EPS = 1e-5
FFN_AT = (0, HID, 2 * HID, (2 + HT) * HID, (2 + 2 * HT) * HID)
FFN_COLS = FFN_AT[4] + HT * M
SCORE_SCALE = 1.0 / D
MASKED = -1e30
QH, QL, KH, KL = range(4)

ROPE_TILES = [(0, 0), (1, 0), (0, 1), (1, 1)]
QK_STEP = (0, 1, 2, 3)
COS_LAG, SIN_LAG, SUM_LAG, HIGH_LAG, LOW_LAG = 1, 1, 2, 3, 3
V_STEP = (4, 5, 6, 7)
PV1_PIECES = {1: range(0, 2), 2: range(2, 4), 3: range(4, 8)}
PV0_PIECES = {6: range(0, 1), 7: range(1, 4)}
ADD0_STEP, ADD1_STEP = 0, 4
LEND1 = (6, 7, 0)
LEND3 = ()
POOL_SUMS = ()
ACT_ORDER = "exp rope high copy v"
DVE_ORDER = "cos inv sum max low add v"
POOL_ORDER = "norm sin sum rope"
FILLS_OF = [1 if i < 4 else 2 for i in range(NI)]
FIRST_FILL = [sum(FILLS_OF[:i]) for i in range(NI)]
NT = sum(FILLS_OF)
NQK, NV = len(QK_STEP), len(V_STEP)
PV_BANK = 7


def plan_banks():
    uses = {}
    last = dict.fromkeys(range(PV_BANK), 0)
    for off in range(2):
        for s in range(NI):
            ib, tile_off = (s + 2) % NI, off + (s + 2) // NI
            first = 2 * (ib % 2)
            uses["s", tile_off, ib] = [first, first + 1] if ib >= 4 else [first]
            lent = [bank for bank, free in ((1, LEND1), (3, LEND3)) if s in free]
            small = [("t", off, FIRST_FILL[s] + k) for k in range(FILLS_OF[s])]
            small += [("qk", off + 1, j) for j in range(NQK) if QK_STEP[j] == s]
            small += [("v", 0, c) for c in range(NV) if off == 0 and V_STEP[c] == s]
            for bank in uses["s", tile_off, ib]:
                last[bank] = len(uses)
            for use in small:
                bank = min([4, 5, 6] + lent, key=lambda b: last[b])
                uses[use] = [bank]
                last[bank] = len(uses)
    return uses


USES = plan_banks()
ORDER = list(USES)


def build(nc, xT, x_tok, w_q, w_k, w_vT, w_o, rope, ident_in, mask_in, f1, f2, g1, g2, f3, scales, out):
    x_split = nc.dram_tensor("x_split", (B, P, 2, T), F32, kind="Internal").ap()
    qk_split = nc.dram_tensor("qk_split", (H, P, 4, P), F32, kind="Internal").ap()
    v_split = nc.dram_tensor("v_split", (H // 2, P, 2, 2 * P), F32, kind="Internal").ap()
    ctx = ExitStack()
    with ctx:
        def sem(name):
            return ctx.enter_context(nc.semaphore(name))

        rT = ctx.enter_context(nc.sbuf_tensor("rT", [P, TOKENS], F32))
        ident = ctx.enter_context(nc.sbuf_tensor("ident", [P, P], F32))
        ffn_raw = ctx.enter_context(nc.sbuf_tensor("ffn_raw", [P, FFN_COLS], F32))
        ffn_loaded = sem("ffn_loaded")
        attn = ctx.enter_context(ExitStack())
        attention(nc, attn, sem, rT, ident, x_split, qk_split, v_split, xT, w_q, w_k, w_vT, w_o, rope, ident_in, mask_in,
                  ffn_raw, (f1, f2, g1, g2, f3), ffn_loaded)
        attn.close()
        feed_forward(nc, ctx, sem, rT, ident, ffn_raw, ffn_loaded, x_tok, scales, out)


def attention(nc, ctx, sem, rT, ident, x_split, qk_split, v_split, xT, w_q, w_k, w_vT, w_o, rope_in, ident_in, mask_in,
              ffn_raw, ffn_weights, ffn_loaded):
    def sb(name, shape, dt=F32, where=ctx):
        return where.enter_context(nc.sbuf_tensor(name, shape, dt))

    rope = sb("rope", [P, 2, T])
    ident_b = sb("ident_b", [P, P], BF16)
    mask_b = sb("mask_b", [P, P], BF16)

    pre = ExitStack()
    raw_x = sb("raw_x", [P, B, T], F32, pre)
    x_parts = sb("x_parts", [P, B, 2, T], F32R, pre)
    qk_parts = sb("qk_parts", [P, H, 4, P], F32R, pre)
    v_parts = sb("v_parts", [P, 2, H * P], F32R, pre)
    raw_w = sb("raw_w", [P, 4, H * P], F32, pre)
    mask_f = sb("mask_f", [P, P], F32, pre)
    warm = sb("warm", [P, 1], F32, pre)
    pvo = pre.enter_context(nc.psum_tensor("pvo", [P, 2 * BANK], F32))

    qk_loaded, vo_loaded, consts_loaded = sem("qk_loaded"), sem("vo_loaded"), sem("consts_loaded")
    x_loaded = [sem(f"x_loaded{b}") for b in range(B)]
    w_high, x_high, x_low, vo_ready = sem("w_high"), sem("x_high"), sem("x_low"), sem("vo_ready")
    saved, warm_zero, w_low = sem("saved"), sem("warm_zero"), sem("w_low")
    with nc.Block() as block:
        @block.sync
        def _(sp):
            sp.dma_start(raw_w[:, 2], w_vT).then_inc(vo_loaded, 16)
            sp.dma_start(raw_w[:, 3], w_o).then_inc(vo_loaded, 16)
            sp.dma_start(raw_w[:, 0], w_q).then_inc(qk_loaded, 16)
            sp.dma_start(raw_w[:, 1], w_k).then_inc(qk_loaded, 16)
            sp.dma_start(ident[:], ident_in).then_inc(consts_loaded, 16)
            sp.dma_start(mask_f[:], mask_in).then_inc(consts_loaded, 16)
            sp.dma_start(rope[:], rope_in).then_inc(consts_loaded, 16)
            def save_x(b):
                sp.wait_ge(x_low, b + 1)
                sp.dma_start(x_split[b], x_parts[:, b].bitcast(F32)).then_inc(saved, 16)

            save_x(0)
            sp.wait_ge(w_low, 1)
            sp.dma_start(qk_split.rearrange("h p k d -> p h k d"), qk_parts[:].bitcast(F32)).then_inc(saved, 16)
            sp.wait_ge(w_low, 2)
            for part in range(2):
                sp.dma_start(v_split[:, :, part].rearrange("h p d -> p h d"),
                             v_parts[:, part].bitcast(F32).rearrange("p (h d) -> p h d", d=2 * P)).then_inc(saved, 16)
            for b in range(1, B):
                save_x(b)
            sp.wait_ge(saved, 16 * (B + 3))

        @block.gpsimd
        def _(pool):
            nc.gpsimd.memset(warm[:], 0.0).then_inc(warm_zero, 1)
            nc.gpsimd.memset(rT[:], 0.0)

        @block.scalar
        def _(act):
            for b in range(B):
                act.dma_start(raw_x[:, b], xT[:, b * T:(b + 1) * T]).then_inc(x_loaded[b], 16)
            act.wait_ge(warm_zero, 1)
            nc.scalar.activation(warm[:], warm[:], ACT.Exp)
            act.wait_ge(x_loaded[0], 16)
            nc.scalar.activation(x_parts[:, 0, 0], raw_x[:, 0], ACT.Copy).then_inc(x_high, 1)
            act.wait_ge(qk_loaded, 32)
            nc.scalar.activation(qk_parts[:, :, QH], raw_w[:, 0].rearrange("p (h d) -> p h d", h=H), ACT.Copy,
                                 scale=SCORE_SCALE).then_inc(w_high, 1)
            nc.scalar.activation(qk_parts[:, :, KH], raw_w[:, 1].rearrange("p (h d) -> p h d", h=H),
                                 ACT.Copy).then_inc(w_high, 1)
            act.wait_ge(vo_ready, 1)
            nc.scalar.activation(v_parts[:, 0], pvo[:], ACT.Copy).then_inc(w_high, 1)
            for b in range(1, B):
                act.wait_ge(x_loaded[b], 16)
                nc.scalar.activation(x_parts[:, b, 0], raw_x[:, b], ACT.Copy).then_inc(x_high, 1)

        @block.tensor
        def _(pe):
            pe.wait_ge(vo_loaded, 32)
            for h in range(H):
                last = nc.tensor.matmul(pvo[:, h * P:(h + 1) * P], raw_w[:, 2, h * P:(h + 1) * P],
                                        raw_w[:, 3, h * P:(h + 1) * P], start=True, stop=True)
            last.then_inc(vo_ready, 1)

        @block.vector
        def _(dve):
            def x_low_part(b):
                dve.wait_ge(x_high, b + 1)
                nc.vector.tensor_tensor(x_parts[:, b, 1], raw_x[:, b], x_parts[:, b, 0].bitcast(F32),
                                        ALU.subtract).then_inc(x_low, 1)

            x_low_part(0)
            dve.wait_ge(w_high, 1)
            nc.vector.scalar_tensor_tensor(qk_parts[:, :, QL], raw_w[:, 0].rearrange("p (h d) -> p h d", h=H),
                                           SCORE_SCALE, qk_parts[:, :, QH].bitcast(F32), ALU.mult, ALU.subtract)
            dve.wait_ge(w_high, 2)
            nc.vector.tensor_tensor(qk_parts[:, :, KL], raw_w[:, 1].rearrange("p (h d) -> p h d", h=H),
                                    qk_parts[:, :, KH].bitcast(F32), ALU.subtract).then_inc(w_low, 1)
            dve.wait_ge(w_high, 3)
            nc.vector.tensor_tensor(v_parts[:, 1], pvo[:], v_parts[:, 0].bitcast(F32), ALU.subtract).then_inc(w_low, 1)
            dve.wait_ge(consts_loaded, 48)
            nc.vector.tensor_copy(ident_b[:], ident[:])
            nc.vector.tensor_copy(mask_b[:], mask_f[:])
            for b in range(1, B):
                x_low_part(b)
    pre.close()

    w_stage = sb("w_stage", [P, 2, 4, P], F32R)
    wv_stage = sb("wv_stage", [P, 2, 2 * P], F32R)
    x_moving = sb("x_moving", [P, 2, 2, T], F32R)
    x_static = sb("x_static", [P, 2, T], F32R)
    qk = sb("qk", [P, 2, 2, 2, T], F32R)
    vals = sb("vals", [P, 2, NI, 2, P], F32R)
    proj = sb("proj", [P, 2, BANK])
    by_cos = sb("by_cos", [P, 2, BANK])
    swapped = sb("swapped", [P, NQK, BANK])
    probs = sb("probs", [P, 4, T])
    pT = [sb("pT0", [P, 2, 4, BANK], F32R), sb("pT1", [P, 2, 8, BANK], F32R)]
    neg_max = sb("neg_max", [P, 2 * NI])
    row_sum = sb("row_sum", [P, 2 * NI])
    inv_sum = sb("inv_sum", [P, 2 * NI])
    psum = ctx.enter_context(nc.psum_tensor("psum", [P, 8 * BANK], F32))
    score_ps = psum[:, :4 * BANK].rearrange("p (s c) -> p s c", s=2)
    pv_ps = psum[:, PV_BANK * BANK:]

    scores_ready = (sem("scores_ready"), NI)
    max_ready = (sem("max_ready"), NI)
    exp_done = (sem("exp_done"), NI)
    inv_ready = (sem("inv_ready"), NI)
    probs_ready = (sem("probs_ready"), NI)
    t_filled = (sem("t_filled"), NT)
    t_high = (sem("t_high"), NT)
    t_low = (sem("t_low"), NT)
    qk_projected = (sem("qk_projected"), NQK)
    proj_copied = (sem("proj_copied"), 4)
    cos_done = (sem("cos_done"), 4)
    sin_done = (sem("sin_done"), 4)
    rope_done = (sem("rope_done"), 4)
    rope_high = (sem("rope_high"), 4)
    rope_low = (sem("rope_low"), 4)
    v_projected = (sem("v_projected"), NV)
    v_high = (sem("v_high"), NV)
    v_low = (sem("v_low"), NV)
    pv_done = (sem("pv_done"), CHUNKS)
    pv_added = (sem("pv_added"), CHUNKS)
    swap_done = [(sem("swap_done0"), 64), (sem("swap_done1"), 64)]
    w_staged = [(sem("w_staged0"), 16), (sem("w_staged1"), 16)]
    wv_staged, x_moved, x_fixed = sem("wv_staged"), sem("x_moved"), sem("x_fixed")
    pool_passed, sp_passed = sem("pool_passed"), sem("sp_passed")

    def number(head):
        return 2 * head[0] + head[1]

    def step_on(head, by):
        return head[0], head[1] + by

    def parity(head):
        return head[1] % 2

    def exists(head):
        n = number(head)
        return not isinstance(n, int) or 0 <= n < HEADS

    def wait_for(eng, signal, head, nth):
        semaphore, each = signal
        if exists(head):
            eng.wait_ge(semaphore, each * number(head) + nth + 1)

    def wait_for_pair(eng, signal, pair, nth):
        if not isinstance(pair, int) or pair >= 0:
            eng.wait_ge(signal[0], signal[1] * pair + nth + 1)

    def wait_for_swap(eng, head, tile):
        if exists(head):
            eng.wait_ge(swap_done[tile % 2][0], 64 * number(head) + 32 * (tile // 2 + 1))

    def earlier(head, nth, by, each):
        return step_on(head, (nth - by) // each), (nth - by) % each

    def run_pairs(eng, body):
        for s in range(NI):
            body((-1, 1), s)
        steps(0, body)
        with eng.Fori(1, PAIRS - 1) as pair:
            steps(pair, body)
        steps(PAIRS - 1, body)
        for s in range(NI):
            body((PAIRS, 0), s)

    def steps(pair, body):
        for off in range(2):
            for s in range(NI):
                body((pair, off), s)

    def rope_tasks(head, s, lag):
        found = []
        for j in range(NQK):
            later, at = divmod(QK_STEP[j] + lag, NI)
            if at == s and exists(step_on(head, 1 - later)):
                found.append((step_on(head, 1 - later), j))
        return found

    def pair_exists(pair):
        return not isinstance(pair, int) or 0 <= pair < PAIRS

    def bank(*use):
        return psum[:, USES[use][0] * BANK:(USES[use][0] + 1) * BANK]

    def wait_for_banks(pe, pair, *use):
        for b in USES[use]:
            at, back = ORDER.index(use), pair
            while True:
                at -= 1
                if at < 0:
                    at, back = len(ORDER) - 1, back - 1
                if isinstance(back, int) and back < -1:
                    break
                kind, off, nth = ORDER[at]
                if b not in USES[ORDER[at]] or not (pair_exists(back) if kind == "v" else exists((back, off))):
                    continue
                if kind == "v":
                    wait_for_pair(pe, v_low, back, nth)
                else:
                    signal = {"t": t_low, "qk": proj_copied, "s": exp_done}[kind]
                    wait_for(pe, signal, (back, off), nth)
                break

    def split_products(out_ap, left, right, first, last):
        terms = ((0, 0), (0, 1), (1, 0))
        for i, (a, b) in enumerate(terms):
            ins = nc.tensor.matmul(out_ap, left[a], right[b], start=first and i == 0, stop=last and i == 2)
        return ins

    def add_rope(eng, engine, head, j):
        wait_for(eng, cos_done, head, j)
        wait_for(eng, sin_done, head, j)
        engine.tensor_tensor(swapped[:, j], by_cos[:, j % 2], swapped[:, j], ALU.add).then_inc(rope_done[0], 1)

    with nc.Block() as block:
        @block.sync
        def _(sp):
            def stage_x(b):
                half = b % 2 if isinstance(b, int) else sp.snap(b % 2)
                src = x_split[b] if isinstance(b, int) else x_split[bass.ds(b, 1)].rearrange("o p a t -> p (o a) t")
                dst = x_moving[:, half] if isinstance(b, int) else x_moving[:, bass.ds(half, 1)].rearrange(
                    "p o a t -> p (o a) t")
                if not isinstance(b, int):
                    sp.wait_ge(qk_projected[0], NQK * H * (b - 1))
                sp.dma_start(dst.bitcast(F32), src).then_inc(x_moved, 16)
                if not isinstance(b, int):
                    sp.wait_ge(v_projected[0], NV * H // 2 * b)
                sp.dma_start(x_static[:].bitcast(F32), src).then_inc(x_fixed, 16)
                sp.wait_ge(x_moved, 16 * b + 16)
                sp.wait_ge(x_fixed, 16 * b + 16)
                sp.sem_inc(sp_passed, 1)

            def stage_pair(b, hp):
                pair = 4 * b + hp
                dynamic = not isinstance(hp, int)
                for q in range(2):
                    head = (pair, q)
                    src = qk_split[bass.ds(sp.snap(2 * hp + q), 1)].rearrange("o p k d -> p (o k) d") if dynamic else \
                        qk_split[2 * hp + q]
                    wait_for(sp, qk_projected, step_on(head, -2), NQK - 1)
                    sp.dma_start(w_stage[:, q].bitcast(F32), src).then_inc(w_staged[q][0], 16)
                    if q == 0:
                        src = v_split[bass.ds(sp.snap(hp + 0), 1)].rearrange("o p k d -> p (o k) d") if dynamic else \
                            v_split[hp]
                        wait_for_pair(sp, v_projected, pair - 1, NV - 1)
                        sp.dma_start(wv_stage[:].bitcast(F32), src).then_inc(wv_staged, 16)
                    for j in range(NQK):
                        wait_for(sp, proj_copied, head, j)
                        for lo, hi in ((0, 64), (64, 0)):
                            sp.dma_start(swapped[lo:lo + 64, j], proj[hi:hi + 64, j % 2]).then_inc(
                                swap_done[j % 2][0], 16)

            stage_x(0)
            for base, src in zip(FFN_AT, ffn_weights):
                sp.dma_start(ffn_raw[:, base:base + src.shape[1]], src).then_inc(ffn_loaded, 16)
            stage_pair(0, 0)
            with sp.Fori(1, H // 2) as hp:
                stage_pair(0, hp)
            with sp.Fori(1, B) as b:
                stage_x(b)
                with sp.Fori(0, H // 2) as hp:
                    stage_pair(b, hp)

        @block.tensor
        def _(pe):
            def scores(head, ib):
                wait_for(pe, rope_low, head, 1 if ib < 4 else 3)
                pair, off = (head[0], head[1]) if (head[1], ib) in [(u[1], u[2]) for u in ORDER if u[0] == "s"] \
                    else (head[0] - 1, head[1] + 2)
                wait_for_banks(pe, pair, "s", off, ib)
                q, k = ([qk[:, parity(head), which, part] for part in range(2)] for which in range(2))
                width = (ib + 1) * P
                for c0 in range(0, width, BANK):
                    cols = slice(c0, min(c0 + BANK, width))
                    dst = score_ps[:, ib % 2, cols]
                    left = [a[:, ib * P:(ib + 1) * P] for a in q]
                    right = [a[:, cols] for a in k]
                    nc.tensor.matmul(dst, left[0], right[0], start=True, stop=False)
                    if cols.stop == width:
                        nc.tensor.matmul(score_ps[:, ib % 2, width - P:width], ident_b[:], mask_b[:],
                                         start=False, stop=False)
                    nc.tensor.matmul(dst, left[0], right[1], start=False, stop=False)
                    last = nc.tensor.matmul(dst, left[1], right[0], start=False, stop=True)
                last.then_inc(scores_ready[0], 1)

            def transpose_probs(head, ib):
                wait_for(pe, probs_ready, head, ib)
                for f in range(FILLS_OF[ib]):
                    nth = FIRST_FILL[ib] + f
                    wait_for_banks(pe, head[0], "t", head[1], nth)
                    for jb in range(4 * f, min(4 * f + 4, ib + 1)):
                        last = nc.tensor.transpose(bank("t", head[1], nth)[:, (jb % 4) * P:(jb % 4 + 1) * P],
                                                   probs[:, ib % 4, jb * P:(jb + 1) * P], ident[:])
                    last.then_inc(t_filled[0], 1)

            def project_qk(running, nth):
                head = step_on(running, 1)
                if nth == 0:
                    pe.wait_ge(w_staged[parity(head)][0], 16 * (head[0] + head[1] // 2) + 16)
                wait_for_banks(pe, running[0], "qk", head[1], nth)
                w = w_stage[:, parity(head)]
                which, c = ROPE_TILES[nth]
                batch_parity = number(head) // H % 2
                if isinstance(batch_parity, int):
                    x = x_moving[:, batch_parity].rearrange("p a t -> p (a t)")
                    x = [x[:, part * T + c * BANK:part * T + (c + 1) * BANK] for part in range(2)]
                else:
                    x = x_moving[:].rearrange("p b a t -> p (b a t)")
                    x = [x[:, bass.ds(batch_parity * (2 * T) + (part * T + c * BANK), BANK)] for part in range(2)]
                split_products(bank("qk", head[1], nth), (w[:, QH + 2 * which], w[:, QL + 2 * which]), x,
                               True, True).then_inc(qk_projected[0], 1)

            def project_v(pair, nth):
                if nth == 0:
                    pe.wait_ge(wv_staged, 16 * pair + 16)
                wait_for_banks(pe, pair, "v", 0, nth)
                for i in range(2):
                    t0 = (2 * nth + i) * P
                    last = split_products(bank("v", 0, nth)[:, i * 2 * P:(i + 1) * 2 * P],
                                          [x_static[:, part, t0:t0 + P] for part in range(2)],
                                          (wv_stage[:, 0], wv_stage[:, 1]), True, True)
                last.then_inc(v_projected[0], 1)

            def attend(head, chunk, key_blocks):
                if key_blocks[0] == 0:
                    wait_for(pe, t_low, head, NT - 1 if chunk else 3)
                    pair = head[0] + head[1] // 2
                    wait_for_pair(pe, v_low, pair, NV - 1 if chunk else 1)
                    wait_for(pe, pv_added, *earlier(head, chunk, 1, CHUNKS))
                for jb in key_blocks:
                    i0 = max(0, jb * P - chunk * BANK)
                    last = split_products(pv_ps[:, i0:], [vals[:, part, jb, parity(head)] for part in range(2)],
                                          [pT[chunk][:, part, jb, i0:] for part in range(2)],
                                          jb == 0, jb == 4 * chunk + 3)
                if key_blocks[-1] == 4 * chunk + 3:
                    last.then_inc(pv_done[0], 1)

            def step(head, s):
                ahead = step_on(head, (s + 2) // NI)
                if exists(ahead):
                    scores(ahead, (s + 2) % NI)
                if exists(head):
                    transpose_probs(head, s)
                for target, j in rope_tasks(head, s, 0):
                    project_qk(step_on(target, -1), j)
                for c in range(NV):
                    if head[1] == 0 and V_STEP[c] == s and exists(head):
                        project_v(head[0], c)
                if s in PV1_PIECES and exists(step_on(head, -1)):
                    attend(step_on(head, -1), 1, PV1_PIECES[s])
                if s in PV0_PIECES and exists(head):
                    attend(head, 0, PV0_PIECES[s])

            run_pairs(pe, step)

        @block.scalar
        def _(act):
            def exponentiate(head, ib):
                n = parity(head) * NI + ib
                wait_for(act, max_ready, head, ib)
                old_head, old = earlier(head, ib, 4, NI)
                wait_for(act, t_filled, old_head, FIRST_FILL[old] + FILLS_OF[old] - 1)
                width = (ib + 1) * P
                nc.scalar.activation(probs[:, ib % 4, :width], score_ps[:, ib % 2, :width], ACT.Exp,
                                     bias=neg_max[:, n:n + 1], accum_out=row_sum[:, n:n + 1]).then_inc(exp_done[0], 1)

            def transposed_high(head, ib):
                chunk = ib // 4
                if ib % 4 == 0:
                    wait_for(act, pv_done, step_on(head, -1), chunk)
                for f in range(FILLS_OF[ib]):
                    nth = FIRST_FILL[ib] + f
                    n_blocks = min(4, ib + 1 - 4 * f)
                    wait_for(act, t_filled, head, nth)
                    nc.scalar.activation(
                        pT[chunk][:, 0, 4 * f:4 * f + n_blocks, (ib % 4) * P:(ib % 4 + 1) * P],
                        bank("t", head[1], nth)[:, :n_blocks * P].rearrange("p (j i) -> p j i", i=P),
                        ACT.Copy).then_inc(t_high[0], 1)

            def copy_projected(head, j):
                wait_for(act, qk_projected, head, j)
                old_head, old = earlier(head, j, 2, 4)
                wait_for(act, cos_done, old_head, old)
                wait_for_swap(act, old_head, old)
                wait_for(act, rope_low, step_on(head, -1), j)
                nc.scalar.activation(proj[:, j % 2], bank("qk", 2 if parity(head) == 0 else 1, j), ACT.Copy).then_inc(proj_copied[0], 1)

            def roped_high(head, j):
                which, c = ROPE_TILES[j]
                wait_for(act, rope_done, head, j)
                if j == 0:
                    wait_for(act, scores_ready, step_on(head, -2), NI - 1)
                nc.scalar.activation(qk[:, parity(head), which, 0, c * BANK:(c + 1) * BANK], swapped[:, j],
                                     ACT.Copy).then_inc(rope_high[0], 1)

            def values_high(pair, nth):
                wait_for_pair(act, v_projected, pair, nth)
                if nth == 0:
                    wait_for(act, pv_done, (pair, -1), 1)
                nc.scalar.activation(vals[:, 0, 2 * nth:2 * nth + 2].rearrange("p j q m -> p (j q m)"),
                                     bank("v", 0, nth), ACT.Copy).then_inc(v_high[0], 1)

            def step(head, s):
                ahead = step_on(head, (s + 1) // NI)
                for what in ACT_ORDER.split():
                    if what == "exp" and exists(ahead):
                        exponentiate(ahead, (s + 1) % NI)
                    if what == "rope":
                        for target, j in rope_tasks(head, s, HIGH_LAG):
                            roped_high(target, j)
                    if what == "high" and exists(head):
                        transposed_high(head, s)
                    if what == "copy":
                        for target, j in rope_tasks(head, s, 0):
                            copy_projected(target, j)
                    if what == "v":
                        for c in range(NV):
                            if head[1] == 0 and V_STEP[c] == s and exists(head):
                                values_high(head[0], c)

            run_pairs(act, step)

        @block.vector
        def _(dve):
            def negative_max(head, ib):
                n = parity(head) * NI + ib
                wait_for(dve, scores_ready, head, ib)
                nc.vector.tensor_reduce(neg_max[:, n:n + 1], score_ps[:, ib % 2, :(ib + 1) * P], AX.X, ALU.max,
                                        negate=True).then_inc(max_ready[0], 1)

            def inverse_sum(head, ib):
                n = parity(head) * NI + ib
                wait_for(dve, exp_done, head, ib)
                nc.vector.reciprocal(inv_sum[:, n:n + 1], row_sum[:, n:n + 1]).then_inc(inv_ready[0], 1)

            def transposed_low(head, ib):
                chunk = ib // 4
                for f in range(FILLS_OF[ib]):
                    nth = FIRST_FILL[ib] + f
                    n_blocks = min(4, ib + 1 - 4 * f)
                    high, low = (pT[chunk][:, part, 4 * f:4 * f + n_blocks, (ib % 4) * P:(ib % 4 + 1) * P]
                                 for part in range(2))
                    wait_for(dve, t_high, head, nth)
                    nc.vector.tensor_tensor(
                        low, bank("t", head[1], nth)[:, :n_blocks * P].rearrange("p (j i) -> p j i", i=P),
                        high.bitcast(F32), ALU.subtract).then_inc(t_low[0], 1)

            def times_cos(head, j):
                c = ROPE_TILES[j][1]
                wait_for(dve, proj_copied, head, j)
                wait_for(dve, rope_done, *earlier(head, j, 2, NQK))
                nc.vector.tensor_tensor(by_cos[:, j % 2], proj[:, j % 2], rope[:, 0, c * BANK:(c + 1) * BANK],
                                        ALU.mult).then_inc(cos_done[0], 1)

            def values_low(pair, nth):
                high, low = (vals[:, part, 2 * nth:2 * nth + 2].rearrange("p j q m -> p (j q m)") for part in range(2))
                wait_for_pair(dve, v_high, pair, nth)
                nc.vector.tensor_tensor(low, bank("v", 0, nth), high.bitcast(F32),
                                        ALU.subtract).then_inc(v_low[0], 1)

            def add_head(head, chunk):
                if not exists(head):
                    return
                col = number(head) // H * T + chunk * BANK
                acc = rT[:, bass.ds(col, BANK)] if not isinstance(col, int) else rT[:, col:col + BANK]
                wait_for(dve, pv_done, head, chunk)
                wait_for(dve, pv_added, *earlier(head, chunk, 2, CHUNKS))
                nc.vector.tensor_tensor(acc, pv_ps[:], acc, ALU.add).then_inc(pv_added[0], 1)

            def step(head, s):
                for what in DVE_ORDER.split():
                    if what == "add" and s == ADD0_STEP:
                        add_head(step_on(head, -1), 0)
                    if what == "add" and s == ADD1_STEP:
                        add_head(step_on(head, -1), 1)
                    if what == "sum":
                        for target, j in rope_tasks(head, s, SUM_LAG):
                            if j not in POOL_SUMS:
                                add_rope(dve, nc.vector, target, j)
                    if what == "cos":
                        for target, j in rope_tasks(head, s, COS_LAG):
                            times_cos(target, j)
                    if what == "inv" and exists(step_on(head, (s + 1) // NI)):
                        inverse_sum(step_on(head, (s + 1) // NI), (s + 1) % NI)
                    if what == "max" and exists(step_on(head, (s + 2) // NI)):
                        negative_max(step_on(head, (s + 2) // NI), (s + 2) % NI)
                    if what == "low" and exists(head):
                        transposed_low(head, s)
                    if what == "v":
                        for c in range(NV):
                            if head[1] == 0 and V_STEP[c] == s and exists(head):
                                values_low(head[0], c)

            run_pairs(dve, step)

        @block.gpsimd
        def _(pool):
            def normalize(head, ib):
                n = parity(head) * NI + ib
                wait_for(pool, inv_ready, head, ib)
                pool.sem_inc(pool_passed, 1)
                p = probs[:, ib % 4, :(ib + 1) * P]
                nc.gpsimd.tensor_scalar(p, p, inv_sum[:, n:n + 1], 1.0, ALU.mult, ALU.mult).then_inc(probs_ready[0], 1)

            def times_sin(head, j):
                c = ROPE_TILES[j][1]
                wait_for_swap(pool, head, j)
                nc.gpsimd.tensor_tensor(swapped[:, j], swapped[:, j], rope[:, 1, c * BANK:(c + 1) * BANK],
                                        ALU.mult).then_inc(sin_done[0], 1)

            def roped_low(head, j):
                which, c = ROPE_TILES[j]
                high, low = (qk[:, parity(head), which, part, c * BANK:(c + 1) * BANK] for part in range(2))
                wait_for(pool, rope_high, head, j)
                nc.gpsimd.tensor_tensor(low, swapped[:, j], high.bitcast(F32), ALU.subtract).then_inc(rope_low[0], 1)

            def step(head, s):
                ahead = step_on(head, (s + 1) // NI)
                for what in POOL_ORDER.split():
                    if what == "norm" and exists(ahead):
                        normalize(ahead, (s + 1) % NI)
                    if what == "sin":
                        for target, j in rope_tasks(head, s, SIN_LAG):
                            times_sin(target, j)
                    if what == "sum":
                        for target, j in rope_tasks(head, s, SUM_LAG):
                            if j in POOL_SUMS:
                                add_rope(pool, nc.gpsimd, target, j)
                    if what == "rope":
                        for target, j in rope_tasks(head, s, LOW_LAG):
                            roped_low(target, j)

            run_pairs(pool, step)


def feed_forward(nc, ctx, sem, rT, ident, raw, ffn_loaded, x_tok, scales_in, out):
    def sb(name, shape, dt=F32):
        return ctx.enter_context(nc.sbuf_tensor(name, shape, dt))

    TWO = TOKENS // (2 * BANK)
    PER = BANK // P
    F1, F2, G1, G2, F3 = FFN_AT
    S1, S2, SG1, SG2, S3 = 0, HT, 2 * HT, 3 * HT, 4 * HT
    RSQRT_STEPS = 3
    RSQRT_SEED = float(0x5F3759DF)
    LINKS = 6 + 3 * RSQRT_STEPS

    w = sb("w", [P, 2, FFN_COLS], F32R)
    scales = sb("scales", [P, 4 * HT + 1])
    y = sb("y", [P, BLOCKS, M])
    r_stage = sb("r_stage", [P, 2, BANK])
    y_norm = sb("y_norm", [P, 2, PER, M])
    yT = sb("yT", [P, 2, 2, BANK], F32R)
    hid = sb("hid", [P, 2, 2, 2, HT, BANK], F32R)
    gate = sb("gate", [P, 2, BANK])
    value = sb("value", [P, 4, BANK])
    outT = sb("outT", [P, 2, BANK])
    norms = []
    for i in range(2):
        norms.append({name: sb(f"{name}{i}", [P, 2 * PER] + more) for name, more in (
            ("stats", [6]), ("mean_var", [2]), ("var", []), ("work", []), ("rstd", []), ("shift", []))})
    ps = ctx.enter_context(nc.psum_tensor("ps", [P, 2, HT, BANK], F32))

    scales_loaded, first_loaded, rest_loaded = sem("scales_loaded"), sem("first_loaded"), sem("rest_loaded")
    w_high, w_low = sem("ffn_w_high"), sem("ffn_w_low")
    r_staged, r_turned, r_added, y_ready, y_kept, y_turned, yT_high, yT_low = (
        (sem(n), 2) for n in ("r_staged", "r_turned", "r_added", "y_ready", "y_kept", "y_turned", "yT_high", "yT_low"))
    gated, gate_done, value_done = ((sem(n), 2 * HT) for n in ("gated", "gate_done", "value_done"))
    layer_done, gelu_done = ((sem(n), 4 * HT) for n in ("layer_done", "gelu_done"))
    hid_high, hid_low = ((sem(n), 6 * HT) for n in ("hid_high", "hid_low"))
    out_filled, out_copied, out_turned, y_summed = (
        (sem(n), 2) for n in ("out_filled", "out_copied", "out_turned", "y_summed"))
    links = [(sem("norm1_link"), LINKS), (sem("norm2_link"), LINKS)]
    out_ready, stored, norm_passed = (sem("out_ready"), 1), sem("stored"), sem("norm_passed")

    def exists(two):
        return not isinstance(two, int) or 0 <= two < TWO

    def wait_for(eng, signal, two, nth):
        if exists(two):
            eng.wait_ge(signal[0], signal[1] * two + nth + 1)

    def run_all(body):
        def run(eng):
            body(-1)
            body(0)
            with eng.Fori(1, TWO - 1) as two:
                body(two)
            body(TWO - 1)
            body(TWO)
        return run

    def w_at(base, part, k, o):
        return w[:, part, base + k + o:base + k + o + P]

    def chunk_of(tensor, two, c):
        if isinstance(two, int):
            return tensor[:, (2 * two + c) * BANK:(2 * two + c + 1) * BANK]
        return tensor[:, bass.ds((2 * two + c) * BANK, BANK)]

    y_flat = y[:].rearrange("p b m -> p (b m)")
    terms = ((0, 0), (0, 1), (1, 0))

    with nc.Block() as block:
        @block.sync
        def _(sp):
            sp.dma_start(y[:, :2 * PER], x_tok[:, :2 * PER]).then_inc(first_loaded, 16)
            sp.dma_start(scales[:], scales_in).then_inc(scales_loaded, 16)
            sp.dma_start(y[:, 2 * PER:], x_tok[:, 2 * PER:]).then_inc(rest_loaded, 16)

            def body(two):
                if exists(two - 1 if isinstance(two, int) else 0):
                    wait_for(sp, out_ready, two - 1, 0)
                    if isinstance(two, int):
                        rows = slice((two - 1) * 2 * PER, two * 2 * PER)
                    else:
                        rows = bass.ds((two - 1) * (2 * PER), 2 * PER)
                    sp.dma_start(out[:, rows], y[:, rows]).then_inc(stored, 16)

            run_all(body)(sp)
            sp.wait_ge(stored, 16 * TWO)

        @block.tensor
        def _(pe):
            def turn_r(two, c):
                wait_for(pe, r_staged, two, c)
                for i in range(PER):
                    last = nc.tensor.transpose(ps[:, 0, c, i * P:(i + 1) * P], r_stage[:, c, i * P:(i + 1) * P], ident[:])
                last.then_inc(r_turned[0], 1)

            def turn_y(two, c):
                wait_for(pe, y_ready, two, c)
                for i in range(PER):
                    last = nc.tensor.transpose(ps[:, 0, c, i * P:(i + 1) * P], y_norm[:, c, i], ident[:])
                last.then_inc(y_turned[0], 1)

            def gated_layer(two):
                for o in range(HT):
                    for c in range(2):
                        if o == 0:
                            wait_for(pe, yT_low, two, c)
                        if o == 1:
                            wait_for(pe, y_summed, two - 1, c)
                        if o >= 2:
                            wait_for(pe, value_done, two, 2 * (o - 2) + c)
                        for n, base in enumerate((F1, F2)):
                            for i, (a, b) in enumerate(terms):
                                last = nc.tensor.matmul(ps[:, c, 2 * ((o + 1) % 2) + n], w_at(base, a, 0, o * P), yT[:, c, b],
                                                        start=i == 0, stop=i == 2)
                        last.then_inc(gated[0], 1)

            def hidden_layer(two, layer, c, middle):
                base = (G1, G2)[layer]
                for k in range(HT):
                    wait_for(pe, hid_low, two, (2 * HT * layer + 2 * k + c) if layer == 0 else (2 + c) * HT + k)
                    if k == 0 and layer == 0:
                        wait_for(pe, value_done, two, 2 * (HT - 1) + c)
                        if isinstance(two, int) and two == 0:
                            pe.wait_ge(w_low, 2)
                    if k == 0 and layer == 1:
                        wait_for(pe, gelu_done, two, c * HT + HT - 1)
                        if c == 0:
                            wait_for(pe, r_added, two + 1, 1)
                        if isinstance(two, int) and two == 0:
                            pe.wait_ge(w_low, 3)
                    if k == 2:
                        middle()
                    for o in range(HT):
                        for i, (a, b) in enumerate(terms):
                            last = nc.tensor.matmul(ps[:, c, o], w_at(base, a, k * HID, o * P), hid[:, c, layer, b, k],
                                                    start=k == 0 and i == 0, stop=k == HT - 1 and i == 2)
                        if k == HT - 1:
                            last.then_inc(layer_done[0], 1)

            def last_layer(two, c):
                if c == 0:
                    wait_for(pe, yT_low, two + 1, 1)
                if isinstance(two, int) and two == 0:
                    pe.wait_ge(w_low, 4)
                for k in range(HT):
                    wait_for(pe, hid_low, two, (4 + c) * HT + k)
                    for i, (a, b) in enumerate(terms):
                        last = nc.tensor.matmul(ps[:, c, 0], w_at(F3, a, k * M, 0), hid[:, c, 0, b, k],
                                                start=k == 0 and i == 0, stop=k == HT - 1 and i == 2)
                last.then_inc(out_filled[0], 1)

            def turn_out(two, c):
                wait_for(pe, out_copied, two, c)
                for i in range(PER):
                    last = nc.tensor.transpose(ps[:, c, 1, i * P:(i + 1) * P], outT[:, c, i * P:(i + 1) * P], ident[:])
                last.then_inc(out_turned[0], 1)

            def ahead(two, turn, layer):
                if exists(two + 1 if isinstance(two, int) else 0):
                    for c in range(2):
                        if exists(two):
                            wait_for(pe, gelu_done, two, 2 * layer * HT + c)
                        elif turn is turn_y:
                            wait_for(pe, r_added, two + 1, c)
                        turn(two + 1, c)

            def body(two):
                if exists(two):
                    if isinstance(two, int) and two == 0:
                        pe.wait_ge(w_low, 1)
                    gated_layer(two)
                    hidden_layer(two, 0, 0, lambda: None)
                    hidden_layer(two, 0, 1, lambda: ahead(two, turn_r, 0))
                    hidden_layer(two, 1, 0, lambda: None)
                    hidden_layer(two, 1, 1, lambda: ahead(two, turn_y, 1))
                    last_layer(two, 0)
                    last_layer(two, 1)
                    turn_out(two, 0)
                    turn_out(two, 1)
                elif two < 0:
                    ahead(two, turn_r, 0)
                    ahead(two, turn_y, 1)

            run_all(body)(pe)

        @block.scalar
        def _(act):
            def body(two):
                def split_y():
                    if exists(two + 1 if isinstance(two, int) else 0):
                        for c in range(2):
                            wait_for(act, y_turned, two + 1, c)
                            nc.scalar.activation(yT[:, c, 0], ps[:, 0, c], ACT.Copy).then_inc(yT_high[0], 1)

                if not exists(two):
                    if two < 0:
                        act.wait_ge(ffn_loaded, 80)
                        for a, b in ((F1, G1), (G1, G2), (G2, F3), (F3, FFN_COLS)):
                            nc.scalar.activation(w[:, 0, a:b], raw[:, a:b], ACT.Copy).then_inc(w_high, 1)
                        act.wait_ge(scales_loaded, 16)
                        split_y()
                    return

                def gated_high(nth):
                    o, c = divmod(nth, 2)
                    wait_for(act, value_done, two, nth)
                    if nth < 2:
                        wait_for(act, out_filled, two - 1, c)
                    nc.scalar.activation(hid[:, c, 0, 0, o], value[:, nth % 4], ACT.Copy).then_inc(hid_high[0], 1)

                for nth in range(2 * HT):
                    o, c = divmod(nth, 2)
                    wait_for(act, gated, two, nth)
                    wait_for(act, value_done, *((two, nth - 2) if nth >= 2 else (two - 1, 2 * HT - 2 + nth)))
                    nc.scalar.activation(gate[:, nth % 2], ps[:, c, 2 * ((o + 1) % 2)], ACT.Silu,
                                         scale=scales[:, S1 + o:S1 + o + 1]).then_inc(gate_done[0], 1)
                    if nth >= 1:
                        gated_high(nth - 1)
                gated_high(2 * HT - 1)
                for layer, at in enumerate((SG1, SG2)):
                    for c in range(2):
                        for o in range(HT):
                            nth = (2 * layer + c) * HT + o
                            wait_for(act, layer_done, two, nth)
                            wait_for(act, hid_low, two, 2 * HT + nth - 4)
                            nc.scalar.activation(value[:, nth % 4], ps[:, c, o], ACT.Gelu,
                                                 scale=scales[:, at + o:at + o + 1]).then_inc(gelu_done[0], 1)
                        if layer == 1 and c == 0:
                            split_y()
                for c in range(2):
                    wait_for(act, out_filled, two, c)
                    nc.scalar.activation(outT[:, c], ps[:, c, 0], ACT.Copy, scale=scales[:, S3:S3 + 1]).then_inc(out_copied[0], 1)

            run_all(body)(act)

        @block.gpsimd
        def _(pool):
            def body(two):
                nxt = two + 1
                if exists(nxt if isinstance(nxt, int) else 0):
                    for c in range(2):
                        wait_for(pool, r_turned, two, c)
                        nc.gpsimd.tensor_copy(r_stage[:, c], chunk_of(rT, nxt, c)).then_inc(r_staged[0], 1)
                if isinstance(two, int) and two < 0:
                    for i, (a, b) in enumerate(((F1, G1), (G1, G2), (G2, F3), (F3, FFN_COLS))):
                        pool.wait_ge(w_high, i + 1)
                        nc.gpsimd.tensor_tensor(w[:, 1, a:b], raw[:, a:b], w[:, 0, a:b].bitcast(F32),
                                                ALU.subtract).then_inc(w_low, 1)
                if exists(nxt if isinstance(nxt, int) else 0):
                    for c in range(2):
                        wait_for(pool, y_ready, nxt, c)
                        nc.gpsimd.tensor_copy(chunk_of(y_flat, nxt, c), y_norm[:, c].rearrange("p b m -> p (b m)")).then_inc(
                            y_kept[0], 1)

            run_all(body)(pool)

        @block.vector
        def _(dve):
            def block_of(two, i):
                if isinstance(two, int):
                    return y[:, two * 2 * PER + i]
                return y[:, bass.ds(two * (2 * PER) + i, 1)].rearrange("p o m -> p (o m)")

            def norm_factors(which, two):
                t = norms[which]
                count = [0]

                def link(ins):
                    ins.then_inc(links[which][0], 1)
                    wait_for(dve, links[which], two, count[0])
                    count[0] += 1

                for i in range(2 * PER):
                    last = nc.vector.bn_stats(t["stats"][:, i], block_of(two, i))
                link(last)
                dve.sem_inc(norm_passed, 1)
                for i in range(2 * PER):
                    last = nc.vector.bn_aggr(t["mean_var"][:, i], t["stats"][:, i])
                link(last)
                var, work, rstd = t["var"][:], t["work"][:], t["rstd"][:]
                link(nc.vector.tensor_scalar(var, t["mean_var"][:, :, 1], EPS, None, ALU.add))
                link(nc.vector.tensor_scalar(work.bitcast(I32), var.bitcast(I32), 1, None, ALU.logical_shift_right))
                link(nc.vector.tensor_scalar(rstd.bitcast(I32), work.bitcast(I32), -1.0, RSQRT_SEED, ALU.mult, ALU.add))
                for _ in range(RSQRT_STEPS):
                    link(nc.vector.scalar_tensor_tensor(work, rstd, -0.5, rstd, ALU.mult, ALU.mult))
                    link(nc.vector.tensor_tensor(work, work, var, ALU.mult))
                    link(nc.vector.scalar_tensor_tensor(rstd, work, 1.5, rstd, ALU.add, ALU.mult))
                link(nc.vector.scalar_tensor_tensor(t["shift"][:], t["mean_var"][:, :, 0], -1.0, rstd, ALU.mult, ALU.mult))
                assert count[0] == LINKS

            def first_norm(two):
                if not exists(two if isinstance(two, int) else 0):
                    return
                t = norms[0]
                for c in range(2):
                    wait_for(dve, r_turned, two, c)
                    part = chunk_of(y_flat, two, c)
                    nc.vector.tensor_tensor(part, ps[:, 0, c], part, ALU.add).then_inc(r_added[0], 1)
                wait_for(dve, r_added, two, 1)
                norm_factors(0, two)
                for c in range(2):
                    wait_for(dve, y_turned, two - 1, c)
                    wait_for(dve, y_kept, two - 1, c)
                    for i in range(c * PER, (c + 1) * PER):
                        last = nc.vector.tensor_scalar(y_norm[:, c, i - c * PER], block_of(two, i), t["rstd"][:, i:i + 1],
                                                       t["shift"][:, i:i + 1], ALU.mult, ALU.add)
                    last.then_inc(y_ready[0], 1)

            def split_y(two):
                if exists(two if isinstance(two, int) else 0):
                    for c in range(2):
                        wait_for(dve, yT_high, two, c)
                        nc.vector.tensor_tensor(yT[:, c, 1], ps[:, 0, c], yT[:, c, 0].bitcast(F32),
                                                ALU.subtract).then_inc(yT_low[0], 1)

            def second_norm(two):
                if not exists(two if isinstance(two, int) else 0):
                    return
                t = norms[1]
                wait_for(dve, y_summed, two, 1)
                norm_factors(1, two)
                for i in range(2 * PER):
                    part = block_of(two, i)
                    last = nc.vector.tensor_scalar(part, part, t["rstd"][:, i:i + 1], t["shift"][:, i:i + 1], ALU.mult, ALU.add)
                last.then_inc(out_ready[0], 1)

            def low(two, c, layer_parity, o, nth):
                wait_for(dve, hid_high, two, nth)
                nc.vector.tensor_tensor(hid[:, c, layer_parity, 1, o], value[:, nth % 4],
                                        hid[:, c, layer_parity, 0, o].bitcast(F32), ALU.subtract).then_inc(hid_low[0], 1)

            def body(two):
                if not exists(two):
                    if two < 0:
                        dve.wait_ge(first_loaded, 16)
                        first_norm(0)
                        split_y(0)
                        dve.wait_ge(scales_loaded, 16)
                        dve.wait_ge(rest_loaded, 16)
                    else:
                        second_norm(TWO - 1)
                    return
                for nth in range(2 * HT):
                    o, c = divmod(nth, 2)
                    wait_for(dve, gate_done, two, nth)
                    wait_for(dve, hid_low, *((two, nth - 4) if nth >= 4 else (two - 1, 6 * HT - 4 + nth)))
                    nc.vector.scalar_tensor_tensor(value[:, nth % 4], ps[:, c, 2 * ((o + 1) % 2) + 1],
                                                   scales[:, S2 + o:S2 + o + 1], gate[:, nth % 2], ALU.mult,
                                                   ALU.mult).then_inc(value_done[0], 1)
                    if nth >= 1:
                        low(two, (nth - 1) % 2, 0, (nth - 1) // 2, nth - 1)
                low(two, 1, 0, HT - 1, 2 * HT - 1)
                second_norm(two - 1)
                for layer in range(2):
                    for c in range(2):
                        for o in range(HT):
                            nth = (2 * layer + c) * HT + o
                            wait_for(dve, gelu_done, two, nth)
                            nc.vector.tensor_copy(hid[:, c, 1 - layer, 0, o], value[:, nth % 4]).then_inc(hid_high[0], 1)
                            low(two, c, 1 - layer, o, 2 * HT + nth)
                        if layer == 0 and c == 0:
                            first_norm(two + 1)
                        if layer == 1 and c == 0:
                            split_y(two + 1)
                for c in range(2):
                    wait_for(dve, out_turned, two, c)
                    wait_for(dve, y_kept, two, c)
                    part = chunk_of(y_flat, two, c)
                    nc.vector.tensor_tensor(part, ps[:, c, 1], part, ALU.add).then_inc(y_summed[0], 1)

            run_all(body)(dve)


def kernel(**inputs):
    import concourse.bacc as bacc
    from concourse.bass_utils import run_bass_kernel_spmd

    def take(name):
        return np.asarray(inputs["L0_" + name])

    def c(a):
        return np.ascontiguousarray(a)

    half = D // 2
    freq = np.power(np.float32(10000.0), -np.arange(half, dtype=np.float32) / np.float32(half)).astype(np.float32)
    angle = (np.arange(T, dtype=np.float32)[None, :] * freq[:, None]).astype(np.float32).astype(np.float64)
    cos, sin = np.cos(angle), np.sin(angle)
    rope = np.stack([np.concatenate([cos, cos]), np.concatenate([-sin, sin])], axis=1).astype(np.float32)

    def by_tile(a, tiles):
        return a.T.reshape(tiles, P, -1).transpose(1, 0, 2).reshape(P, -1)

    x = take("attn_x").reshape(TOKENS, M)
    scales = np.concatenate([take(n).reshape(-1, P).T for n in ("ffn_w1_s", "ffn_w2_s", "ffn_h1_s", "ffn_h2_s", "ffn_w3_s")], axis=1)
    arrays = {
        "xT": c(x.T),
        "x_tok": c(x.reshape(BLOCKS, P, M).transpose(1, 0, 2)),
        "w_q": c(take("attn_w_aq").reshape(M, H * D)),
        "w_k": c(take("attn_w_ak").reshape(M, H * D)),
        "w_vT": c(take("attn_w_av").transpose(2, 1, 0).reshape(D, H * M)),
        "w_o": c(take("attn_w_ao").transpose(1, 0, 2).reshape(D, H * M)),
        "rope_in": rope,
        "ident_in": np.eye(P, dtype=np.float32),
        "mask_in": np.triu(np.full((P, P), MASKED, np.float32), 1),
        "f1": c(by_tile(take("ffn_w1_w"), 1)),
        "f2": c(by_tile(take("ffn_w2_w"), 1)),
        "g1": c(by_tile(take("ffn_h1_w"), HT)),
        "g2": c(by_tile(take("ffn_h2_w"), HT)),
        "f3": c(by_tile(take("ffn_w3_w"), HT)),
        "scales_in": c(scales),
    }
    nc = bacc.Bacc("TRN2", target_bir_lowering=False, num_devices=1)
    args = [nc.dram_tensor(n, a.shape, mybir.dt.from_np(a.dtype), kind="ExternalInput").ap() for n, a in arrays.items()]
    out = nc.dram_tensor("out", (P, BLOCKS, M), F32, kind="ExternalOutput").ap()
    build(nc, *args, out)
    r = run_bass_kernel_spmd(nc, [arrays], core_ids=[0])
    return r.results[0]["out"].transpose(1, 0, 2).reshape(B, T, M)
```

```python
from contextlib import ExitStack

import concourse.bass as bass
import numpy as np
from concourse import mybir

F32 = mybir.dt.float32
F32R = mybir.dt.float32r
BF16 = mybir.dt.bfloat16
I32 = mybir.dt.int32
ACT = mybir.ActivationFunctionType
ALU = mybir.AluOpType
AX = mybir.AxisListType

B, T, M = 4, 1024, 128
H, D = 8, 128
HID = 512
P = 128
BANK = 512
HEADS = B * H
PAIRS = HEADS // 2
NI = T // P
CHUNKS = T // BANK
TOKENS = B * T
BLOCKS = TOKENS // P
HT = HID // P
EPS = 1e-5
FFN_AT = (0, HID, 2 * HID, (2 + HT) * HID, (2 + 2 * HT) * HID)
FFN_COLS = FFN_AT[4] + HT * M
SCORE_SCALE = 1.0 / D
MASKED = -1e30
QH, QL, KH, KL = range(4)

ROPE_TILES = [(0, 0), (1, 0), (0, 1), (1, 1)]
QK_STEP = (0, 0, 2, 2)
COS_STEP = (1, 2, 3, 4)
SIN_STEP = (1, 2, 3, 4)
SUM_STEP = (2, 3, 4, 6)
HIGH_STEP = (3, 4, 6, 8)
LOW_STEP = (3, 4, 6, 8)
V_STEP = (4, 5, 6, 6)
PV0_PIECES = {6: range(0, 2), 7: range(2, 4)}
PV1_PIECES = {1: range(0, 2), 2: range(2, 4), 3: range(4, 8)}
ADD0_STEP, ADD1_STEP = 0, 4
LEND1 = (6, 7, 0)
LEND3 = (1, 2)
FILLS_OF = [1 if i < 4 else 2 for i in range(NI)]
FIRST_FILL = [sum(FILLS_OF[:i]) for i in range(NI)]
NT = sum(FILLS_OF)
NQK, NV = len(QK_STEP), len(V_STEP)
PV_BANK = 7


def plan_banks():
    uses = {}
    last = dict.fromkeys(range(PV_BANK), 0)
    for off in range(2):
        for s in range(NI):
            ib, tile_off = (s + 2) % NI, off + (s + 2) // NI
            first = 2 * (ib % 2)
            lent = [bank for bank, free in ((1, LEND1), (3, LEND3)) if s in free]
            after = ([("t", off, FIRST_FILL[s] + k) for k in range(FILLS_OF[s])]
                     + [("qk", off + 1, j) for j in range(NQK) if QK_STEP[j] == s]
                     + [("v", 0, c) for c in range(NV) if V_STEP[c] == NI * off + s])
            for use in [("s", tile_off, ib)] + after:
                if use[0] == "s":
                    uses[use] = [first, first + 1] if ib >= 4 else [first]
                else:
                    uses[use] = [min([4, 5, 6] + lent, key=lambda b: last[b])]
                for bank in uses[use]:
                    last[bank] = len(uses)
    return uses


USES = plan_banks()
ORDER = list(USES)


def build(nc, xT, x_tok, w_q, w_k, w_vT, w_o, rope, ident_in, mask_in, f1, f2, g1, g2, f3, scales, out):
    x_split = nc.dram_tensor("x_split", (B - 2, P, 2, T), F32, kind="Internal").ap()
    qk_split = nc.dram_tensor("qk_split", (H, P, 4, P), F32, kind="Internal").ap()
    v_split = nc.dram_tensor("v_split", (H // 2, P, 2, 2 * P), F32, kind="Internal").ap()
    ctx = ExitStack()
    with ctx:
        def sem(name):
            return ctx.enter_context(nc.semaphore(name))

        rT = ctx.enter_context(nc.sbuf_tensor("rT", [P, TOKENS], F32))
        ident = ctx.enter_context(nc.sbuf_tensor("ident", [P, P], F32))
        ffn_raw = ctx.enter_context(nc.sbuf_tensor("ffn_raw", [P, FFN_COLS], F32))
        ffn_loaded = sem("ffn_loaded")
        attn = ctx.enter_context(ExitStack())
        attention(nc, attn, sem, rT, ident, x_split, qk_split, v_split, xT, w_q, w_k, w_vT, w_o, rope, ident_in, mask_in,
                  ffn_raw, (f1, f2, g1, g2, f3), ffn_loaded)
        attn.close()
        feed_forward(nc, ctx, sem, rT, ident, ffn_raw, ffn_loaded, x_tok, scales, out)


def attention(nc, ctx, sem, rT, ident, x_split, qk_split, v_split, xT, w_q, w_k, w_vT, w_o, rope_in, ident_in, mask_in,
              ffn_raw, ffn_weights, ffn_loaded):
    def sb(name, shape, dt=F32, where=ctx):
        return where.enter_context(nc.sbuf_tensor(name, shape, dt))

    rope = sb("rope", [P, 2, T])
    ident_b = sb("ident_b", [P, P], BF16)
    mask_b = sb("mask_b", [P, P], BF16)
    w_stage = sb("w_stage", [P, 2, 4, P], F32R)
    wv_stage = sb("wv_stage", [P, 2, 2 * P], F32R)
    x_moving = sb("x_moving", [P, 2, 2, T], F32R)
    x_static = sb("x_static", [P, 2, T], F32R)
    qk = sb("qk", [P, 2, 2, 2, T], F32R)
    proj = sb("proj", [P, 2, BANK])
    by_cos = sb("by_cos", [P, 2, BANK])
    swapped = sb("swapped", [P, NQK, BANK])

    pre = ExitStack()
    raw_x = sb("raw_x", [P, B, T], F32, pre)
    raw_w = sb("raw_w", [P, 4, H * P], F32, pre)
    qk_parts = sb("qk_parts", [P, H - 2, 4, P], F32R, pre)
    v_parts = sb("v_parts", [P, 2, H * P], F32R, pre)
    mask_f = sb("mask_f", [P, P], F32, pre)
    warm = sb("warm", [P, 1], F32, pre)
    pre.close()
    x_parts = ffn_raw[:, :(B - 2) * 2 * T].bitcast(F32R).rearrange("p (b a t) -> p b a t", b=B - 2, a=2)
    probs = sb("probs", [P, 4, T])
    pT0 = sb("pT0", [P, 2, 4, BANK], F32R)
    pT = [pT0, sb("pT1", [P, 2, 8, BANK], F32R)]
    vals = sb("vals", [P, 2, NI, 2, P], F32R)
    neg_max = sb("neg_max", [P, 2 * NI])
    row_sum = sb("row_sum", [P, 2 * NI])
    inv_sum = sb("inv_sum", [P, 2 * NI])
    psum = ctx.enter_context(nc.psum_tensor("psum", [P, 8 * BANK], F32))
    score_ps = psum[:, :4 * BANK].rearrange("p (s h c) -> p s h c", s=2, h=2)
    pv_ps = psum[:, PV_BANK * BANK:]
    taken = {b for j in range(NQK) for b in USES["qk", 2, j]}
    vo_bank = next(b for b in range(PV_BANK) if not taken & {b, b + 1})
    vo_ps = psum[:, vo_bank * BANK:(vo_bank + 2) * BANK]

    weight_parts = ((slice(0, 2), w_stage), (slice(2, H), qk_parts))
    qk_loaded, vo_loaded, consts_loaded = sem("qk_loaded"), sem("vo_loaded"), sem("consts_loaded")
    x_loaded = [sem(f"x_loaded{b}") for b in range(B)]
    qk_high, qk_low, x_high, x_low = sem("qk_w_high"), sem("qk_w_low"), sem("x_high"), sem("x_low")
    vo_ready, vo_high, vo_low = sem("vo_ready"), sem("vo_high"), sem("vo_low")
    w_saved, x_saved, warm_zero = sem("w_saved"), sem("x_saved"), sem("warm_zero")
    r_zero, masks_ready = sem("r_zero"), sem("masks_ready")
    W_SAVED, X_SAVED = 16 * (len(weight_parts) + 2), 16 * (B - 2)

    scores_ready = (sem("scores_ready"), NI)
    max_ready = (sem("max_ready"), NI)
    exp_done = (sem("exp_done"), NI)
    inv_ready = (sem("inv_ready"), NI)
    probs_ready = (sem("probs_ready"), NI)
    t_filled = (sem("t_filled"), NT)
    t_high = (sem("t_high"), NT)
    t_low = (sem("t_low"), NT)
    qk_projected = (sem("qk_projected"), NQK)
    proj_copied = (sem("proj_copied"), 4)
    cos_done = (sem("cos_done"), 4)
    sin_done = (sem("sin_done"), 4)
    rope_done = (sem("rope_done"), 4)
    rope_high = (sem("rope_high"), 4)
    rope_low = (sem("rope_low"), 4)
    v_projected = (sem("v_projected"), NV)
    v_high = (sem("v_high"), NV)
    v_low = (sem("v_low"), NV)
    pv_done = (sem("pv_done"), CHUNKS)
    pv_added = (sem("pv_added"), CHUNKS)
    swap_done = [(sem("swap_done0"), 64), (sem("swap_done1"), 64)]
    w_staged = [(sem("w_staged0"), 16), (sem("w_staged1"), 16)]
    wv_staged, x_fixed = sem("wv_staged"), sem("x_fixed")
    x_moved = sem("x_moved")
    pool_passed = sem("pool_passed")

    def score_halves(ib):
        width = (ib + 1) * P
        return (1, width) if width <= BANK else (2, width // 2)

    def x_part(b, part):
        return x_moving[:, b, part] if b < 2 else x_parts[:, b - 2, part]

    def number(head):
        return 2 * head[0] + head[1]

    def step_on(head, by):
        return head[0], head[1] + by

    def parity(head):
        return head[1] % 2

    def exists(head):
        n = number(head)
        return not isinstance(n, int) or 0 <= n < HEADS

    def wait_for(eng, signal, head, nth):
        semaphore, each = signal
        if exists(head):
            eng.wait_ge(semaphore, each * number(head) + nth + 1)

    def wait_for_pair(eng, signal, pair, nth):
        if not isinstance(pair, int) or pair >= 0:
            eng.wait_ge(signal[0], signal[1] * pair + nth + 1)

    def wait_for_swap(eng, head, tile):
        if exists(head):
            eng.wait_ge(swap_done[tile % 2][0], 64 * number(head) + 32 * (tile // 2 + 1))

    def earlier(head, nth, by, each):
        return step_on(head, (nth - by) // each), (nth - by) % each

    def run_pairs(eng, body):
        for s in range(NI):
            body((-1, 1), s)
        steps(0, body)
        with eng.Fori(1, PAIRS - 1) as pair:
            steps(pair, body)
        steps(PAIRS - 1, body)
        for s in range(NI):
            body((PAIRS, 0), s)

    def steps(pair, body):
        for off in range(2):
            for s in range(NI):
                body((pair, off), s)

    def rope_tasks(head, s, steps):
        found = []
        for j in range(NQK):
            later, at = divmod(steps[j], NI)
            if at == s and exists(step_on(head, 1 - later)):
                found.append((step_on(head, 1 - later), j))
        return found

    def v_tasks(head, s):
        return [c for c in range(NV) if V_STEP[c] == NI * head[1] + s and exists(head)]

    def is_first(head):
        return isinstance(head[0], int) and number(head) == 0

    def before_first(head):
        return isinstance(head[0], int) and head[0] < 0

    def pair_exists(pair):
        return not isinstance(pair, int) or 0 <= pair < PAIRS

    def bank(*use):
        return psum[:, USES[use][0] * BANK:(USES[use][0] + 1) * BANK]

    def wait_for_banks(pe, pair, *use):
        for b in USES[use]:
            at, back = ORDER.index(use), pair
            while True:
                at -= 1
                if at < 0:
                    at, back = len(ORDER) - 1, back - 1
                if isinstance(back, int) and back < -1:
                    break
                kind, off, nth = ORDER[at]
                if b not in USES[ORDER[at]] or not (pair_exists(back) if kind == "v" else exists((back, off))):
                    continue
                if kind == "v":
                    wait_for_pair(pe, v_low, back, nth)
                else:
                    signal = {"t": t_low, "qk": proj_copied, "s": exp_done}[kind]
                    wait_for(pe, signal, (back, off), nth)
                break

    def split_products(out_ap, left, right, first, last):
        terms = ((0, 0), (0, 1), (1, 0))
        for i, (a, b) in enumerate(terms):
            ins = nc.tensor.matmul(out_ap, left[a], right[b], start=first and i == 0, stop=last and i == 2)
        return ins

    with nc.Block() as block:
        @block.sync
        def _(sp):
            sp.dma_start(raw_w[:, 0], w_q).then_inc(qk_loaded, 16)
            sp.dma_start(raw_w[:, 1], w_k).then_inc(qk_loaded, 16)
            sp.dma_start(rope[:], rope_in).then_inc(consts_loaded, 16)
            sp.dma_start(mask_f[:], mask_in).then_inc(consts_loaded, 16)
            sp.dma_start(ident[:], ident_in).then_inc(consts_loaded, 16)
            for b in range(1, B):
                sp.dma_start(raw_x[:, b], xT[:, b * T:(b + 1) * T]).then_inc(x_loaded[b], 16)

            def half_of(b):
                if isinstance(b, int):
                    return x_moving[:, b % 2]
                return x_moving[:, bass.ds(sp.snap(b % 2), 1)].rearrange("p o a t -> p (o a) t")

            def stage_x_moving(b):
                dst = half_of(b)
                src = x_split[b - 2] if isinstance(b, int) else x_split[bass.ds(sp.snap(b - 2), 1)].rearrange(
                    "o p a t -> p (o a) t")
                sp.wait_ge(qk_projected[0], NQK * H * (b - 1))
                sp.wait_ge(x_fixed, 16 * b)
                sp.dma_start(dst.bitcast(F32), src).then_inc(x_moved, 16)

            def stage_pair(b, hp):
                pair = H // 2 * b + hp
                dynamic = not isinstance(hp, int)
                first = isinstance(pair, int) and pair == 0

                def stage_for_values():
                    src = v_parts[:, :, :2 * P].bitcast(F32) if first else v_split[hp] if not dynamic else \
                        v_split[bass.ds(sp.snap(hp + 0), 1)].rearrange("o p k d -> p (o k) d")
                    x_half = None if dynamic else half_of(b)
                    wait_for_pair(sp, v_projected, pair - 1, NV - 1)
                    if first:
                        sp.wait_ge(vo_low, 1)
                        sp.wait_ge(x_moved, 16)
                    if not dynamic:
                        sp.dma_start(x_static[:].bitcast(F32), x_half.bitcast(F32)).then_inc(x_fixed, 16)
                    sp.dma_start(wv_stage[:].bitcast(F32), src).then_inc(wv_staged, 16)

                for q in range(2):
                    head = (pair, q)
                    src = qk_split[bass.ds(sp.snap(2 * hp + q), 1)].rearrange("o p k d -> p (o k) d") if dynamic else \
                        qk_split[2 * hp + q]
                    if not first:
                        wait_for(sp, qk_projected, step_on(head, -2), NQK - 1)
                        sp.dma_start(w_stage[:, q].bitcast(F32), src).then_inc(w_staged[q][0], 16)
                    if q == 0 and not first:
                        stage_for_values()
                    for j in range(NQK):
                        wait_for(sp, proj_copied, head, j)
                        for lo, hi in ((0, 64), (64, 0)):
                            sp.dma_start(swapped[lo:lo + 64, j], proj[hi:hi + 64, j % 2]).then_inc(
                                swap_done[j % 2][0], 16)
                    if q == 0 and first:
                        stage_for_values()

            def stage_batch(b):
                stage_pair(b, 0)
                if not isinstance(b, int) or 1 <= b < B - 1:
                    stage_x_moving(b + 1)
                with sp.Fori(1, H // 2) as hp:
                    stage_pair(b, hp)

            stage_pair(0, 0)
            sp.wait_ge(w_saved, W_SAVED)
            with sp.Fori(1, H // 2) as hp:
                stage_pair(0, hp)
            sp.wait_ge(x_saved, X_SAVED)
            for base, src in zip(FFN_AT, ffn_weights):
                sp.dma_start(ffn_raw[:, base:base + src.shape[1]], src).then_inc(ffn_loaded, 16)
            with sp.Fori(1, B - 1) as b:
                stage_batch(b)
            stage_batch(B - 1)

        @block.tensor
        def _(pe):
            def scores(head, ib):
                wait_for(pe, rope_low, head, 1 if ib < 4 else 3)
                pair, off = head if ("s", head[1], ib) in USES else (head[0] - 1, head[1] + 2)
                wait_for_banks(pe, pair, "s", off, ib)
                q, k = ([qk[:, parity(head), which, part] for part in range(2)] for which in range(2))
                halves, half = score_halves(ib)
                for h in range(halves):
                    dst = score_ps[:, ib % 2, h, :half]
                    left = [a[:, ib * P:(ib + 1) * P] for a in q]
                    right = [a[:, h * half:(h + 1) * half] for a in k]
                    nc.tensor.matmul(dst, left[0], right[0], start=True, stop=False)
                    if h == halves - 1:
                        nc.tensor.matmul(dst[:, half - P:], ident_b[:], mask_b[:], start=False, stop=False)
                    nc.tensor.matmul(dst, left[0], right[1], start=False, stop=False)
                    last = nc.tensor.matmul(dst, left[1], right[0], start=False, stop=True)
                last.then_inc(scores_ready[0], 1)

            def transpose_probs(head, ib):
                wait_for(pe, probs_ready, head, ib)
                for f in range(FILLS_OF[ib]):
                    nth = FIRST_FILL[ib] + f
                    wait_for_banks(pe, head[0], "t", head[1], nth)
                    for jb in range(4 * f, min(4 * f + 4, ib + 1)):
                        last = nc.tensor.transpose(bank("t", head[1], nth)[:, (jb % 4) * P:(jb % 4 + 1) * P],
                                                   probs[:, ib % 4, jb * P:(jb + 1) * P], ident[:])
                    last.then_inc(t_filled[0], 1)

            def project_qk(running, nth):
                head = step_on(running, 1)
                if nth == 0:
                    pe.wait_ge(w_staged[parity(head)][0], 16 * (head[0] + head[1] // 2) + 16)
                    pe.wait_ge(x_moved, 16 * (number(head) // H) + 16)
                wait_for_banks(pe, running[0], "qk", head[1], nth)
                w = w_stage[:, parity(head)]
                which, c = ROPE_TILES[nth]
                batch_parity = number(head) // H % 2
                if isinstance(batch_parity, int):
                    x = x_moving[:, batch_parity].rearrange("p a t -> p (a t)")
                    x = [x[:, part * T + c * BANK:part * T + (c + 1) * BANK] for part in range(2)]
                else:
                    x = x_moving[:].rearrange("p b a t -> p (b a t)")
                    x = [x[:, bass.ds(batch_parity * (2 * T) + (part * T + c * BANK), BANK)] for part in range(2)]
                split_products(bank("qk", head[1], nth), (w[:, QH + 2 * which], w[:, QL + 2 * which]), x,
                               True, True).then_inc(qk_projected[0], 1)

            def project_v(pair, nth):
                if nth == 0:
                    pe.wait_ge(wv_staged, 16 * pair + 16)
                    pe.wait_ge(x_fixed, 16 * (2 * pair // H) + 16)
                wait_for_banks(pe, pair, "v", 0, nth)
                for i in range(2):
                    t0 = (2 * nth + i) * P
                    last = split_products(bank("v", 0, nth)[:, i * 2 * P:(i + 1) * 2 * P],
                                          [x_static[:, part, t0:t0 + P] for part in range(2)],
                                          (wv_stage[:, 0], wv_stage[:, 1]), True, True)
                last.then_inc(v_projected[0], 1)

            def attend(head, chunk, key_blocks):
                if key_blocks[0] == 0:
                    wait_for(pe, t_low, head, NT - 1 if chunk else 3)
                    pair = head[0] + head[1] // 2
                    wait_for_pair(pe, v_low, pair, NV - 1 if chunk else 1)
                    wait_for(pe, pv_added, *earlier(head, chunk, 1, CHUNKS))
                for jb in key_blocks:
                    i0 = max(0, jb * P - chunk * BANK)
                    last = split_products(pv_ps[:, i0:], [vals[:, part, jb, parity(head)] for part in range(2)],
                                          [pT[chunk][:, part, jb, i0:] for part in range(2)],
                                          jb == 0, jb == 4 * chunk + 3)
                if key_blocks[-1] == 4 * chunk + 3:
                    last.then_inc(pv_done[0], 1)

            def step(head, s):
                ahead = step_on(head, (s + 2) // NI)
                if before_first(head) and s == 1:
                    pe.wait_ge(vo_loaded, 32)
                    for h in range(H):
                        last = nc.tensor.matmul(vo_ps[:, h * P:(h + 1) * P], raw_w[:, 2, h * P:(h + 1) * P],
                                                raw_w[:, 3, h * P:(h + 1) * P], start=True, stop=True)
                    last.then_inc(vo_ready, 1)
                if before_first(head) and s == NI - 2:
                    pe.wait_ge(masks_ready, 1)
                    pe.wait_ge(vo_low, 1)
                if exists(ahead):
                    scores(ahead, (s + 2) % NI)
                if exists(head):
                    transpose_probs(head, s)
                for target, j in rope_tasks(head, s, QK_STEP):
                    project_qk(step_on(target, -1), j)
                for c in v_tasks(head, s):
                    project_v(head[0], c)
                if s in PV0_PIECES and exists(head):
                    attend(head, 0, PV0_PIECES[s])
                if s in PV1_PIECES and exists(step_on(head, -1)):
                    attend(step_on(head, -1), 1, PV1_PIECES[s])

            run_pairs(pe, step)

        @block.scalar
        def _(act):
            act.dma_start(raw_x[:, 0], xT[:, :T]).then_inc(x_loaded[0], 16)
            act.dma_start(raw_w[:, 2], w_vT).then_inc(vo_loaded, 16)
            act.dma_start(raw_w[:, 3], w_o).then_inc(vo_loaded, 16)
            act.wait_ge(warm_zero, 1)
            nc.scalar.activation(warm[:], warm[:], ACT.Exp)

            def high_of_x(b):
                act.wait_ge(x_loaded[b], 16)
                nc.scalar.activation(x_part(b, 0), raw_x[:, b], ACT.Copy).then_inc(x_high, 1)

            high_of_x(0)
            act.wait_ge(qk_loaded, 32)
            for heads, parts in weight_parts:
                raw_q, raw_k = (raw_w[:, i].rearrange("p (h d) -> p h d", h=H)[:, heads] for i in range(2))
                nc.scalar.activation(parts[:, :, QH], raw_q, ACT.Copy, scale=SCORE_SCALE).then_inc(qk_high, 1)
                nc.scalar.activation(parts[:, :, KH], raw_k, ACT.Copy).then_inc(qk_high, 1)

            def save_x(b):
                act.wait_ge(x_low, b + 1)
                act.dma_start(x_split[b - 2], x_parts[:, b - 2].bitcast(F32)).then_inc(x_saved, 16)

            def save_weights():
                for nth, (heads, parts) in enumerate(weight_parts):
                    act.wait_ge(qk_low, nth + 1)
                    act.dma_start(qk_split[heads].rearrange("h p k d -> p h k d"),
                                  parts[:].bitcast(F32)).then_inc(w_saved, 16)
                act.wait_ge(vo_low, 1)
                for part in range(2):
                    act.dma_start(v_split[:, :, part].rearrange("h p d -> p h d"),
                                  v_parts[:, part].bitcast(F32).rearrange("p (h d) -> p h d", d=2 * P)).then_inc(
                                      w_saved, 16)

            def exponentiate(head, ib):
                n = parity(head) * NI + ib
                wait_for(act, max_ready, head, ib)
                old_head, old = earlier(head, ib, 4, NI)
                wait_for(act, t_filled, old_head, FIRST_FILL[old] + FILLS_OF[old] - 1)
                width = (ib + 1) * P
                halves, half = score_halves(ib)
                nc.scalar.activation(probs[:, ib % 4, :width].rearrange("p (h c) -> p h c", h=halves),
                                     score_ps[:, ib % 2, :halves, :half], ACT.Exp,
                                     bias=neg_max[:, n:n + 1], accum_out=row_sum[:, n:n + 1]).then_inc(exp_done[0], 1)

            def transposed_high(head, ib):
                chunk = ib // 4
                if ib % 4 == 0:
                    wait_for(act, pv_done, step_on(head, -1), chunk)
                for f in range(FILLS_OF[ib]):
                    nth = FIRST_FILL[ib] + f
                    n_blocks = min(4, ib + 1 - 4 * f)
                    wait_for(act, t_filled, head, nth)
                    nc.scalar.activation(
                        pT[chunk][:, 0, 4 * f:4 * f + n_blocks, (ib % 4) * P:(ib % 4 + 1) * P],
                        bank("t", head[1], nth)[:, :n_blocks * P].rearrange("p (j i) -> p j i", i=P),
                        ACT.Copy).then_inc(t_high[0], 1)

            def copy_projected(head, j):
                wait_for(act, qk_projected, head, j)
                old_head, old = earlier(head, j, 2, 4)
                wait_for(act, cos_done, old_head, old)
                wait_for_swap(act, old_head, old)
                wait_for(act, rope_low, step_on(head, -1), j)
                nc.scalar.activation(proj[:, j % 2], bank("qk", 1 if parity(head) else 2, j),
                                     ACT.Copy).then_inc(proj_copied[0], 1)

            def roped_high(head, j):
                which, c = ROPE_TILES[j]
                wait_for(act, rope_done, head, j)
                if j == 0:
                    wait_for(act, scores_ready, step_on(head, -2), NI - 1)
                nc.scalar.activation(qk[:, parity(head), which, 0, c * BANK:(c + 1) * BANK], swapped[:, j],
                                     ACT.Copy).then_inc(rope_high[0], 1)

            def values_high(pair, nth):
                wait_for_pair(act, v_projected, pair, nth)
                if nth == 0:
                    wait_for(act, pv_done, (pair, -1), 1)
                nc.scalar.activation(vals[:, 0, 2 * nth:2 * nth + 2].rearrange("p j q m -> p (j q m)"),
                                     bank("v", 0, nth), ACT.Copy).then_inc(v_high[0], 1)

            def step(head, s):
                ahead = step_on(head, (s + 1) // NI)
                if before_first(head) and s == 1:
                    act.wait_ge(vo_ready, 1)
                    nc.scalar.activation(v_parts[:, 0], vo_ps, ACT.Copy).then_inc(vo_high, 1)
                if before_first(head) and s == 4:
                    for b in range(1, B):
                        high_of_x(b)
                if before_first(head) and s == NI - 2:
                    save_weights()
                if before_first(head) and s == NI - 1:
                    act.wait_ge(vo_low, 1)
                    act.wait_ge(x_low, B)
                    act.wait_ge(masks_ready, 1)
                if is_first(head) and s == NI - 1:
                    for b in range(2, B):
                        save_x(b)
                if is_first(head) and s == 4:
                    act.wait_ge(w_saved, W_SAVED)
                    act.wait_ge(wv_staged, 16)
                if exists(ahead):
                    exponentiate(ahead, (s + 1) % NI)
                for target, j in rope_tasks(head, s, HIGH_STEP):
                    roped_high(target, j)
                if exists(head):
                    transposed_high(head, s)
                for target, j in rope_tasks(head, s, QK_STEP):
                    copy_projected(target, j)
                for c in v_tasks(head, s):
                    values_high(head[0], c)

            run_pairs(act, step)

        @block.vector
        def _(dve):
            def low_of_x(b):
                dve.wait_ge(x_high, b + 1)
                ins = nc.vector.tensor_tensor(x_part(b, 1), raw_x[:, b], x_part(b, 0).bitcast(F32), ALU.subtract)
                ins.then_inc(x_low, 1)
                if b < 2:
                    dve.wait_ge(x_low, b + 1)
                    dve.sem_inc(x_moved, 16)

            low_of_x(0)
            for nth, (heads, parts) in enumerate(weight_parts):
                dve.wait_ge(qk_high, 2 * nth + 1)
                raw_q, raw_k = (raw_w[:, i].rearrange("p (h d) -> p h d", h=H)[:, heads] for i in range(2))
                nc.vector.scalar_tensor_tensor(parts[:, :, QL], raw_q, SCORE_SCALE,
                                               parts[:, :, QH].bitcast(F32), ALU.mult, ALU.subtract)
                dve.wait_ge(qk_high, 2 * nth + 2)
                nc.vector.tensor_tensor(parts[:, :, KL], raw_k, parts[:, :, KH].bitcast(F32),
                                        ALU.subtract).then_inc(qk_low, 1)
                if nth == 0:
                    dve.wait_ge(qk_low, 1)
                    for buffer in range(2):
                        dve.sem_inc(w_staged[buffer][0], 16)
            dve.wait_ge(consts_loaded, 48)

            def negative_max(head, ib):
                n = parity(head) * NI + ib
                wait_for(dve, scores_ready, head, ib)
                halves, half = score_halves(ib)
                nc.vector.tensor_reduce(neg_max[:, n:n + 1], score_ps[:, ib % 2, :halves, :half], AX.XY, ALU.max,
                                        negate=True).then_inc(max_ready[0], 1)

            def inverse_sum(head, ib):
                n = parity(head) * NI + ib
                wait_for(dve, exp_done, head, ib)
                nc.vector.reciprocal(inv_sum[:, n:n + 1], row_sum[:, n:n + 1]).then_inc(inv_ready[0], 1)

            def transposed_low(head, ib):
                chunk = ib // 4
                for f in range(FILLS_OF[ib]):
                    nth = FIRST_FILL[ib] + f
                    n_blocks = min(4, ib + 1 - 4 * f)
                    high, low = (pT[chunk][:, part, 4 * f:4 * f + n_blocks, (ib % 4) * P:(ib % 4 + 1) * P]
                                 for part in range(2))
                    wait_for(dve, t_high, head, nth)
                    nc.vector.tensor_tensor(
                        low, bank("t", head[1], nth)[:, :n_blocks * P].rearrange("p (j i) -> p j i", i=P),
                        high.bitcast(F32), ALU.subtract).then_inc(t_low[0], 1)

            def times_cos(head, j):
                c = ROPE_TILES[j][1]
                wait_for(dve, proj_copied, head, j)
                wait_for(dve, rope_done, *earlier(head, j, 2, NQK))
                nc.vector.tensor_tensor(by_cos[:, j % 2], proj[:, j % 2], rope[:, 0, c * BANK:(c + 1) * BANK],
                                        ALU.mult).then_inc(cos_done[0], 1)

            def rope_sum(head, j):
                wait_for(dve, sin_done, head, j)
                wait_for(dve, cos_done, head, j)
                nc.vector.tensor_tensor(swapped[:, j], by_cos[:, j % 2], swapped[:, j], ALU.add).then_inc(rope_done[0], 1)

            def values_low(pair, nth):
                high, low = (vals[:, part, 2 * nth:2 * nth + 2].rearrange("p j q m -> p (j q m)") for part in range(2))
                wait_for_pair(dve, v_high, pair, nth)
                nc.vector.tensor_tensor(low, bank("v", 0, nth), high.bitcast(F32),
                                        ALU.subtract).then_inc(v_low[0], 1)

            def add_head(head, chunk):
                if not exists(head):
                    return
                col = number(head) // H * T + chunk * BANK
                acc = rT[:, bass.ds(col, BANK)] if not isinstance(col, int) else rT[:, col:col + BANK]
                if is_first(head):
                    dve.wait_ge(r_zero, 1)
                wait_for(dve, pv_done, head, chunk)
                wait_for(dve, pv_added, *earlier(head, chunk, 2, CHUNKS))
                nc.vector.tensor_tensor(acc, pv_ps[:], acc, ALU.add).then_inc(pv_added[0], 1)

            def step(head, s):
                if before_first(head) and s == 3:
                    dve.wait_ge(vo_high, 1)
                    nc.vector.tensor_tensor(v_parts[:, 1], vo_ps, v_parts[:, 0].bitcast(F32),
                                            ALU.subtract).then_inc(vo_low, 1)
                    nc.vector.tensor_copy(ident_b[:], ident[:])
                    nc.vector.tensor_copy(mask_b[:], mask_f[:]).then_inc(masks_ready, 1)
                if before_first(head) and s == 5:
                    for b in range(1, B):
                        low_of_x(b)
                for target, j in rope_tasks(head, s, COS_STEP):
                    times_cos(target, j)
                if exists(step_on(head, (s + 1) // NI)):
                    inverse_sum(step_on(head, (s + 1) // NI), (s + 1) % NI)
                for target, j in rope_tasks(head, s, SUM_STEP):
                    rope_sum(target, j)
                if exists(step_on(head, (s + 2) // NI)):
                    negative_max(step_on(head, (s + 2) // NI), (s + 2) % NI)
                if s == ADD0_STEP:
                    add_head(step_on(head, -1), 0)
                if s == ADD1_STEP:
                    add_head(step_on(head, -1), 1)
                if exists(head):
                    transposed_low(head, s)
                for c in v_tasks(head, s):
                    values_low(head[0], c)

            run_pairs(dve, step)

        @block.gpsimd
        def _(pool):
            nc.gpsimd.memset(warm[:], 0.0).then_inc(warm_zero, 1)
            nc.gpsimd.memset(rT[:], 0.0).then_inc(r_zero, 1)
            pool.wait_ge(consts_loaded, 48)

            def normalize(head, ib):
                n = parity(head) * NI + ib
                wait_for(pool, inv_ready, head, ib)
                pool.sem_inc(pool_passed, 1)
                p = probs[:, ib % 4, :(ib + 1) * P]
                nc.gpsimd.tensor_scalar(p, p, inv_sum[:, n:n + 1], 1.0, ALU.mult, ALU.mult).then_inc(probs_ready[0], 1)

            def times_sin(head, j):
                c = ROPE_TILES[j][1]
                wait_for_swap(pool, head, j)
                nc.gpsimd.tensor_tensor(swapped[:, j], swapped[:, j], rope[:, 1, c * BANK:(c + 1) * BANK],
                                        ALU.mult).then_inc(sin_done[0], 1)

            def roped_low(head, j):
                which, c = ROPE_TILES[j]
                high, low = (qk[:, parity(head), which, part, c * BANK:(c + 1) * BANK] for part in range(2))
                wait_for(pool, rope_high, head, j)
                nc.gpsimd.tensor_tensor(low, swapped[:, j], high.bitcast(F32), ALU.subtract).then_inc(rope_low[0], 1)

            def step(head, s):
                ahead = step_on(head, (s + 1) // NI)
                if exists(ahead):
                    normalize(ahead, (s + 1) % NI)
                for target, j in rope_tasks(head, s, SIN_STEP):
                    times_sin(target, j)
                for target, j in rope_tasks(head, s, LOW_STEP):
                    roped_low(target, j)

            run_pairs(pool, step)


def feed_forward(nc, ctx, sem, rT, ident, raw, ffn_loaded, x_tok, scales_in, out):
    def sb(name, shape, dt=F32):
        return ctx.enter_context(nc.sbuf_tensor(name, shape, dt))

    TWO = TOKENS // (2 * BANK)
    PER = BANK // P
    F1, F2, G1, G2, F3 = FFN_AT
    S1, S2, SG1, SG2, S3 = 0, HT, 2 * HT, 3 * HT, 4 * HT
    RSQRT_STEPS = 3
    RSQRT_SEED = float(0x5F3759DF)
    LINKS = 6 + 3 * RSQRT_STEPS

    w = sb("w", [P, 2, FFN_COLS], F32R)
    scales = sb("scales", [P, 4 * HT + 1])
    y = sb("y", [P, BLOCKS, M])
    r_stage = sb("r_stage", [P, 2, BANK])
    y_norm = sb("y_norm", [P, 2, PER, M])
    yT = sb("yT", [P, 2, 2, BANK], F32R)
    hid = sb("hid", [P, 2, 2, 2, HT, BANK], F32R)
    gate = sb("gate", [P, 2, BANK])
    value = sb("value", [P, 4, BANK])
    outT = sb("outT", [P, 2, BANK])
    norms = []
    for i in range(2):
        norms.append({name: sb(f"{name}{i}", [P, 2 * PER] + more) for name, more in (
            ("stats", [6]), ("mean_var", [2]), ("var", []), ("work", []), ("rstd", []), ("shift", []))})
    ps = ctx.enter_context(nc.psum_tensor("ps", [P, 2, HT, BANK], F32))

    scales_loaded, first_loaded, rest_loaded = sem("scales_loaded"), sem("first_loaded"), sem("rest_loaded")
    w_high, w_low = sem("ffn_w_high"), sem("ffn_w_low")
    r_staged, r_turned, r_added, y_ready, y_kept, y_turned, yT_high, yT_low = (
        (sem(n), 2) for n in ("r_staged", "r_turned", "r_added", "y_ready", "y_kept", "y_turned", "yT_high", "yT_low"))
    gated, gate_done, value_done = ((sem(n), 2 * HT) for n in ("gated", "gate_done", "value_done"))
    layer_done, gelu_done = ((sem(n), 4 * HT) for n in ("layer_done", "gelu_done"))
    hid_high, hid_low = ((sem(n), 6 * HT) for n in ("hid_high", "hid_low"))
    out_filled, out_copied, out_turned, y_summed = (
        (sem(n), 2) for n in ("out_filled", "out_copied", "out_turned", "y_summed"))
    links = [(sem("norm1_link"), LINKS), (sem("norm2_link"), LINKS)]
    out_ready, stored, norm_passed = (sem("out_ready"), 1), sem("stored"), sem("norm_passed")

    def exists(two):
        return not isinstance(two, int) or 0 <= two < TWO

    def wait_for(eng, signal, two, nth):
        if exists(two):
            eng.wait_ge(signal[0], signal[1] * two + nth + 1)

    def run_all(body):
        def run(eng):
            body(-1)
            body(0)
            with eng.Fori(1, TWO - 1) as two:
                body(two)
            body(TWO - 1)
            body(TWO)
        return run

    def gate_ps(o, c, which):
        return ps[:, c, 2 * ((o + 1) % 2) + which]

    def w_at(base, part, k, o):
        return w[:, part, base + k + o:base + k + o + P]

    def chunk_of(tensor, two, c):
        if isinstance(two, int):
            return tensor[:, (2 * two + c) * BANK:(2 * two + c + 1) * BANK]
        return tensor[:, bass.ds((2 * two + c) * BANK, BANK)]

    y_flat = y[:].rearrange("p b m -> p (b m)")
    terms = ((0, 0), (0, 1), (1, 0))

    with nc.Block() as block:
        @block.sync
        def _(sp):
            sp.dma_start(y[:, :2 * PER], x_tok[:, :2 * PER]).then_inc(first_loaded, 16)
            sp.dma_start(scales[:], scales_in).then_inc(scales_loaded, 16)
            sp.dma_start(y[:, 2 * PER:], x_tok[:, 2 * PER:]).then_inc(rest_loaded, 16)

            def body(two):
                if exists(two - 1 if isinstance(two, int) else 0):
                    wait_for(sp, out_ready, two - 1, 0)
                    if isinstance(two, int):
                        rows = slice((two - 1) * 2 * PER, two * 2 * PER)
                    else:
                        rows = bass.ds((two - 1) * (2 * PER), 2 * PER)
                    sp.dma_start(out[:, rows], y[:, rows]).then_inc(stored, 16)

            run_all(body)(sp)
            sp.wait_ge(stored, 16 * TWO)

        @block.tensor
        def _(pe):
            def turn_r(two, c):
                if isinstance(two, int) and two == 0:
                    src = rT[:, c * BANK:(c + 1) * BANK]
                else:
                    wait_for(pe, r_staged, two, c)
                    src = r_stage[:, c]
                for i in range(PER):
                    last = nc.tensor.transpose(ps[:, 0, c, i * P:(i + 1) * P], src[:, i * P:(i + 1) * P], ident[:])
                last.then_inc(r_turned[0], 1)

            def turn_y(two, c):
                wait_for(pe, y_ready, two, c)
                for i in range(PER):
                    last = nc.tensor.transpose(ps[:, 0, c, i * P:(i + 1) * P], y_norm[:, c, i], ident[:])
                last.then_inc(y_turned[0], 1)

            def gated_layer(two):
                for o in range(HT):
                    for c in range(2):
                        if o == 0:
                            wait_for(pe, yT_low, two, c)
                        if o == 1:
                            wait_for(pe, y_summed, two - 1, c)
                        if o >= 2:
                            wait_for(pe, value_done, two, 2 * (o - 2) + c)
                        for n, base in enumerate((F1, F2)):
                            for i, (a, b) in enumerate(terms):
                                last = nc.tensor.matmul(gate_ps(o, c, n), w_at(base, a, 0, o * P), yT[:, c, b],
                                                        start=i == 0, stop=i == 2)
                        last.then_inc(gated[0], 1)

            def hidden_layer(two, layer, c, middle):
                base = (G1, G2)[layer]
                for k in range(HT):
                    wait_for(pe, hid_low, two, (2 * HT * layer + 2 * k + c) if layer == 0 else (2 + c) * HT + k)
                    if k == 0 and layer == 0:
                        if isinstance(two, int) and two == 0:
                            pe.wait_ge(w_low, 2)
                    if k == 0 and layer == 1:
                        wait_for(pe, gelu_done, two, c * HT + HT - 1)
                        if c == 0:
                            wait_for(pe, r_added, two + 1, 1)
                        if isinstance(two, int) and two == 0:
                            pe.wait_ge(w_low, 3)
                    if k == 2:
                        middle()
                    for o in (2, 3, 0, 1) if k == 0 and layer == 0 else range(HT):
                        if k == 0 and layer == 0 and o in (0, 2):
                            wait_for(pe, value_done, two, 2 * (HT - (1 if o == 0 else 2)) + c)
                        for i, (a, b) in enumerate(terms):
                            last = nc.tensor.matmul(ps[:, c, o], w_at(base, a, k * HID, o * P), hid[:, c, layer, b, k],
                                                    start=k == 0 and i == 0, stop=k == HT - 1 and i == 2)
                        if k == HT - 1:
                            last.then_inc(layer_done[0], 1)

            def last_layer(two, c):
                if c == 0:
                    wait_for(pe, yT_low, two + 1, 1)
                if isinstance(two, int) and two == 0:
                    pe.wait_ge(w_low, 4)
                for k in range(HT):
                    wait_for(pe, hid_low, two, (4 + c) * HT + k)
                    for i, (a, b) in enumerate(terms):
                        last = nc.tensor.matmul(ps[:, c, 0], w_at(F3, a, k * M, 0), hid[:, c, 0, b, k],
                                                start=k == 0 and i == 0, stop=k == HT - 1 and i == 2)
                last.then_inc(out_filled[0], 1)

            def turn_out(two, c):
                wait_for(pe, out_copied, two, c)
                for i in range(PER):
                    last = nc.tensor.transpose(ps[:, c, 1, i * P:(i + 1) * P], outT[:, c, i * P:(i + 1) * P], ident[:])
                last.then_inc(out_turned[0], 1)

            def ahead(two, turn, layer):
                if exists(two + 1 if isinstance(two, int) else 0):
                    for c in range(2):
                        if exists(two):
                            wait_for(pe, gelu_done, two, 2 * layer * HT + c)
                        elif turn is turn_y:
                            wait_for(pe, r_added, two + 1, c)
                        turn(two + 1, c)

            def body(two):
                if exists(two):
                    if isinstance(two, int) and two == 0:
                        pe.wait_ge(w_low, 1)
                    gated_layer(two)
                    hidden_layer(two, 0, 0, lambda: None)
                    hidden_layer(two, 0, 1, lambda: ahead(two, turn_r, 0))
                    hidden_layer(two, 1, 0, lambda: None)
                    hidden_layer(two, 1, 1, lambda: ahead(two, turn_y, 1))
                    last_layer(two, 0)
                    last_layer(two, 1)
                    turn_out(two, 0)
                    turn_out(two, 1)
                elif two < 0:
                    ahead(two, turn_r, 0)
                    ahead(two, turn_y, 1)

            run_all(body)(pe)

        @block.scalar
        def _(act):
            def body(two):
                def split_y():
                    if exists(two + 1 if isinstance(two, int) else 0):
                        for c in range(2):
                            wait_for(act, y_turned, two + 1, c)
                            nc.scalar.activation(yT[:, c, 0], ps[:, 0, c], ACT.Copy).then_inc(yT_high[0], 1)

                if not exists(two):
                    if two < 0:
                        act.wait_ge(ffn_loaded, 80)
                        for a, b in ((F1, G1), (G1, G2), (G2, F3), (F3, FFN_COLS)):
                            nc.scalar.activation(w[:, 0, a:b], raw[:, a:b], ACT.Copy).then_inc(w_high, 1)
                        act.wait_ge(scales_loaded, 16)
                        split_y()
                    return

                def gated_high(nth):
                    o, c = divmod(nth, 2)
                    wait_for(act, value_done, two, nth)
                    if nth < 2:
                        wait_for(act, out_filled, two - 1, c)
                    nc.scalar.activation(hid[:, c, 0, 0, o], value[:, nth % 4], ACT.Copy).then_inc(hid_high[0], 1)

                for nth in range(2 * HT):
                    o, c = divmod(nth, 2)
                    wait_for(act, gated, two, nth)
                    wait_for(act, value_done, *((two, nth - 2) if nth >= 2 else (two - 1, 2 * HT - 2 + nth)))
                    nc.scalar.activation(gate[:, nth % 2], gate_ps(o, c, 0), ACT.Silu,
                                         scale=scales[:, S1 + o:S1 + o + 1]).then_inc(gate_done[0], 1)
                    if nth >= 1:
                        gated_high(nth - 1)
                gated_high(2 * HT - 1)
                for layer, at in enumerate((SG1, SG2)):
                    for c in range(2):
                        for o in range(HT):
                            nth = (2 * layer + c) * HT + o
                            wait_for(act, layer_done, two, nth)
                            wait_for(act, hid_low, two, 2 * HT + nth - 4)
                            nc.scalar.activation(value[:, nth % 4], ps[:, c, o], ACT.Gelu,
                                                 scale=scales[:, at + o:at + o + 1]).then_inc(gelu_done[0], 1)
                        if layer == 1 and c == 0:
                            split_y()
                for c in range(2):
                    wait_for(act, out_filled, two, c)
                    nc.scalar.activation(outT[:, c], ps[:, c, 0], ACT.Copy,
                                         scale=scales[:, S3:S3 + 1]).then_inc(out_copied[0], 1)

            run_all(body)(act)

        @block.gpsimd
        def _(pool):
            def body(two):
                nxt = two + 1
                if isinstance(two, int) and two < 0:
                    pool.sem_inc(r_staged[0], 2)
                elif exists(nxt if isinstance(nxt, int) else 0):
                    for c in range(2):
                        wait_for(pool, r_turned, two, c)
                        nc.gpsimd.tensor_copy(r_stage[:, c], chunk_of(rT, nxt, c)).then_inc(r_staged[0], 1)
                if isinstance(two, int) and two < 0:
                    for i, (a, b) in enumerate(((F1, G1), (G1, G2), (G2, F3), (F3, FFN_COLS))):
                        pool.wait_ge(w_high, i + 1)
                        nc.gpsimd.tensor_tensor(w[:, 1, a:b], raw[:, a:b], w[:, 0, a:b].bitcast(F32),
                                                ALU.subtract).then_inc(w_low, 1)
                if exists(nxt if isinstance(nxt, int) else 0):
                    for c in range(2):
                        wait_for(pool, y_ready, nxt, c)
                        nc.gpsimd.tensor_copy(chunk_of(y_flat, nxt, c),
                                              y_norm[:, c].rearrange("p b m -> p (b m)")).then_inc(y_kept[0], 1)

            run_all(body)(pool)

        @block.vector
        def _(dve):
            def block_of(two, i):
                if isinstance(two, int):
                    return y[:, two * 2 * PER + i]
                return y[:, bass.ds(two * (2 * PER) + i, 1)].rearrange("p o m -> p (o m)")

            def norm_factors(which, two):
                t = norms[which]
                count = [0]

                def link(ins):
                    ins.then_inc(links[which][0], 1)
                    wait_for(dve, links[which], two, count[0])
                    count[0] += 1

                for i in range(2 * PER):
                    last = nc.vector.bn_stats(t["stats"][:, i], block_of(two, i))
                link(last)
                dve.sem_inc(norm_passed, 1)
                for i in range(2 * PER):
                    last = nc.vector.bn_aggr(t["mean_var"][:, i], t["stats"][:, i])
                link(last)
                var, work, rstd = t["var"][:], t["work"][:], t["rstd"][:]
                link(nc.vector.tensor_scalar(var, t["mean_var"][:, :, 1], EPS, None, ALU.add))
                link(nc.vector.tensor_scalar(work.bitcast(I32), var.bitcast(I32), 1, None, ALU.logical_shift_right))
                link(nc.vector.tensor_scalar(rstd.bitcast(I32), work.bitcast(I32), -1.0, RSQRT_SEED, ALU.mult, ALU.add))
                for _ in range(RSQRT_STEPS):
                    link(nc.vector.scalar_tensor_tensor(work, rstd, -0.5, rstd, ALU.mult, ALU.mult))
                    link(nc.vector.tensor_tensor(work, work, var, ALU.mult))
                    link(nc.vector.scalar_tensor_tensor(rstd, work, 1.5, rstd, ALU.add, ALU.mult))
                link(nc.vector.scalar_tensor_tensor(t["shift"][:], t["mean_var"][:, :, 0], -1.0, rstd,
                                                    ALU.mult, ALU.mult))
                assert count[0] == LINKS

            def first_norm(two):
                if not exists(two if isinstance(two, int) else 0):
                    return
                t = norms[0]
                for c in range(2):
                    wait_for(dve, r_turned, two, c)
                    part = chunk_of(y_flat, two, c)
                    nc.vector.tensor_tensor(part, ps[:, 0, c], part, ALU.add).then_inc(r_added[0], 1)
                wait_for(dve, r_added, two, 1)
                norm_factors(0, two)
                for c in range(2):
                    wait_for(dve, y_turned, two - 1, c)
                    wait_for(dve, y_kept, two - 1, c)
                    for i in range(c * PER, (c + 1) * PER):
                        last = nc.vector.tensor_scalar(y_norm[:, c, i - c * PER], block_of(two, i), t["rstd"][:, i:i + 1],
                                                       t["shift"][:, i:i + 1], ALU.mult, ALU.add)
                    last.then_inc(y_ready[0], 1)

            def split_y(two):
                if exists(two if isinstance(two, int) else 0):
                    for c in range(2):
                        wait_for(dve, yT_high, two, c)
                        nc.vector.tensor_tensor(yT[:, c, 1], ps[:, 0, c], yT[:, c, 0].bitcast(F32),
                                                ALU.subtract).then_inc(yT_low[0], 1)

            def second_norm(two):
                if not exists(two if isinstance(two, int) else 0):
                    return
                t = norms[1]
                wait_for(dve, y_summed, two, 1)
                norm_factors(1, two)
                for i in range(2 * PER):
                    part = block_of(two, i)
                    last = nc.vector.tensor_scalar(part, part, t["rstd"][:, i:i + 1], t["shift"][:, i:i + 1],
                                                   ALU.mult, ALU.add)
                last.then_inc(out_ready[0], 1)

            def low(two, c, layer_parity, o, nth):
                wait_for(dve, hid_high, two, nth)
                nc.vector.tensor_tensor(hid[:, c, layer_parity, 1, o], value[:, nth % 4],
                                        hid[:, c, layer_parity, 0, o].bitcast(F32), ALU.subtract).then_inc(hid_low[0], 1)

            def body(two):
                if not exists(two):
                    if two < 0:
                        dve.wait_ge(first_loaded, 16)
                        first_norm(0)
                        split_y(0)
                        dve.wait_ge(scales_loaded, 16)
                        dve.wait_ge(rest_loaded, 16)
                    else:
                        second_norm(TWO - 1)
                    return
                for nth in range(2 * HT):
                    o, c = divmod(nth, 2)
                    wait_for(dve, gate_done, two, nth)
                    wait_for(dve, hid_low, *((two, nth - 4) if nth >= 4 else (two - 1, 6 * HT - 4 + nth)))
                    nc.vector.scalar_tensor_tensor(value[:, nth % 4], gate_ps(o, c, 1),
                                                   scales[:, S2 + o:S2 + o + 1], gate[:, nth % 2], ALU.mult,
                                                   ALU.mult).then_inc(value_done[0], 1)
                    if nth >= 1:
                        low(two, (nth - 1) % 2, 0, (nth - 1) // 2, nth - 1)
                low(two, 1, 0, HT - 1, 2 * HT - 1)
                second_norm(two - 1)
                for layer in range(2):
                    for c in range(2):
                        for o in range(HT):
                            nth = (2 * layer + c) * HT + o
                            wait_for(dve, gelu_done, two, nth)
                            nc.vector.tensor_copy(hid[:, c, 1 - layer, 0, o], value[:, nth % 4]).then_inc(hid_high[0], 1)
                            low(two, c, 1 - layer, o, 2 * HT + nth)
                        if layer == 0 and c == 0:
                            first_norm(two + 1)
                        if layer == 1 and c == 0:
                            split_y(two + 1)
                for c in range(2):
                    wait_for(dve, out_turned, two, c)
                    wait_for(dve, y_kept, two, c)
                    part = chunk_of(y_flat, two, c)
                    nc.vector.tensor_tensor(part, ps[:, c, 1], part, ALU.add).then_inc(y_summed[0], 1)

            run_all(body)(dve)


def kernel(**inputs):
    import concourse.bacc as bacc
    from concourse.bass_utils import run_bass_kernel_spmd

    def take(name):
        return np.asarray(inputs["L0_" + name])

    def c(a):
        return np.ascontiguousarray(a)

    half = D // 2
    freq = np.power(np.float32(10000.0), -np.arange(half, dtype=np.float32) / np.float32(half)).astype(np.float32)
    angle = (np.arange(T, dtype=np.float32)[None, :] * freq[:, None]).astype(np.float32).astype(np.float64)
    cos, sin = np.cos(angle), np.sin(angle)
    rope = np.stack([np.concatenate([cos, cos]), np.concatenate([-sin, sin])], axis=1).astype(np.float32)

    def by_tile(a, tiles):
        return a.T.reshape(tiles, P, -1).transpose(1, 0, 2).reshape(P, -1)

    x = take("attn_x").reshape(TOKENS, M)
    scales = np.concatenate([take(n).reshape(-1, P).T for n in
                             ("ffn_w1_s", "ffn_w2_s", "ffn_h1_s", "ffn_h2_s", "ffn_w3_s")], axis=1)
    arrays = {
        "xT": c(x.T),
        "x_tok": c(x.reshape(BLOCKS, P, M).transpose(1, 0, 2)),
        "w_q": c(take("attn_w_aq").reshape(M, H * D)),
        "w_k": c(take("attn_w_ak").reshape(M, H * D)),
        "w_vT": c(take("attn_w_av").transpose(2, 1, 0).reshape(D, H * M)),
        "w_o": c(take("attn_w_ao").transpose(1, 0, 2).reshape(D, H * M)),
        "rope_in": rope,
        "ident_in": np.eye(P, dtype=np.float32),
        "mask_in": np.triu(np.full((P, P), MASKED, np.float32), 1),
        "f1": c(by_tile(take("ffn_w1_w"), 1)),
        "f2": c(by_tile(take("ffn_w2_w"), 1)),
        "g1": c(by_tile(take("ffn_h1_w"), HT)),
        "g2": c(by_tile(take("ffn_h2_w"), HT)),
        "f3": c(by_tile(take("ffn_w3_w"), HT)),
        "scales_in": c(scales),
    }
    nc = bacc.Bacc("TRN2", target_bir_lowering=False, num_devices=1)
    args = [nc.dram_tensor(n, a.shape, mybir.dt.from_np(a.dtype), kind="ExternalInput").ap() for n, a in arrays.items()]
    out = nc.dram_tensor("out", (P, BLOCKS, M), F32, kind="ExternalOutput").ap()
    build(nc, *args, out)
    r = run_bass_kernel_spmd(nc, [arrays], core_ids=[0])
    return r.results[0]["out"].transpose(1, 0, 2).reshape(B, T, M)
```
